# Optimizing a Trainium2 kernel written in Bass

```python
import numpy as np
import jax
import jax.numpy as jnp

def _softmax(x, axis=-1):
    return jax.nn.softmax(x, axis=axis)

def _gelu(x):
    return jax.nn.gelu(x, approximate=True)

def _silu(x):
    return jax.nn.silu(x)

def _sigmoid(x):
    return jax.nn.sigmoid(x)

def _layernorm(x, axis=-1, eps=1e-05):
    m = jnp.mean(x, axis=axis, keepdims=True)
    v = jnp.var(x, axis=axis, keepdims=True)
    return (x - m) / jnp.sqrt(v + eps)

def _scatter_add(tgt, idx, src, axis=0):
    return tgt.at[idx].add(src)

def _segment_sum(src, seg, n):
    return jax.ops.segment_sum(src, seg, n)
kernel_name = 'mk_macaron_d1_jaxref_r8_6e67dc'

def setup_inputs(seed: int=0):
    np.random.seed(seed)
    _w = jnp.asarray

    def _L0_attn_setup():
        import jax, jax.numpy as jnp
        import numpy as np
        import math
        B, S, D_IN, D_KQ, D_OUT = (4, 256, 128, 128, 128)
        key = jax.random.key(seed)
        ks = jax.random.split(key, 7)
        sc = 0.02
        return {'x': jax.random.normal(ks[0], (B, S, D_IN), jnp.float32), 'Wq': jax.random.normal(ks[1], (D_KQ, D_IN), jnp.float32) * sc, 'bq': jax.random.normal(ks[2], (D_KQ,), jnp.float32) * sc, 'Wk': jax.random.normal(ks[3], (D_KQ, D_IN), jnp.float32) * sc, 'bk': jax.random.normal(ks[4], (D_KQ,), jnp.float32) * sc, 'Wv': jax.random.normal(ks[5], (D_OUT, D_IN), jnp.float32) * sc, 'bv': jax.random.normal(ks[6], (D_OUT,), jnp.float32) * sc}
    _L0_attn_in = _L0_attn_setup()

    def _L0_ffn_setup():
        import jax, jax.numpy as jnp
        import numpy as np
        N_HEADS = 4
        key = jax.random.key(seed)
        k1, k2, k3, k4 = jax.random.split(key, 4)
        dmodel, n_experts, expert_size = (128, 64, 128)
        B, S = (4, 256)
        x = jax.random.normal(k1, (B, S, dmodel), dtype=jnp.float32)
        expert_sel = jax.random.normal(k2, (n_experts, dmodel), dtype=jnp.float32) * dmodel ** (-0.5)
        keys = jax.random.normal(k3, (n_experts, dmodel, expert_size), dtype=jnp.float32) * dmodel ** (-0.5)
        values = jax.random.normal(k4, (n_experts, expert_size, dmodel), dtype=jnp.float32) * (n_experts * expert_size) ** (-0.5)
        return {'x': x, 'expert_sel': expert_sel, 'keys': keys, 'values': values}
    _L0_ffn_in = _L0_ffn_setup()
    _d = {'L0_attn_x': _L0_attn_in['x'], 'L0_attn_Wq': _L0_attn_in['Wq'], 'L0_attn_bq': _L0_attn_in['bq'], 'L0_attn_Wk': _L0_attn_in['Wk'], 'L0_attn_bk': _L0_attn_in['bk'], 'L0_attn_Wv': _L0_attn_in['Wv'], 'L0_attn_bv': _L0_attn_in['bv'], 'L0_ffn_expert_sel': _L0_ffn_in['expert_sel'], 'L0_ffn_keys': _L0_ffn_in['keys'], 'L0_ffn_values': _L0_ffn_in['values']}
    _x0 = _d['L0_attn_x']
    _d['L0_attn_x'] = jax.random.normal(jax.random.fold_in(jax.random.key(seed), 1), (4, 1024, 128), dtype=_x0.dtype)
    del _x0
    return _d

def reference(L0_attn_x, L0_attn_Wq, L0_attn_bq, L0_attn_Wk, L0_attn_bk, L0_attn_Wv, L0_attn_bv, L0_ffn_expert_sel, L0_ffn_keys, L0_ffn_values):

    def _L0_attn_ref(x, Wq, bq, Wk, bk, Wv, bv):
        import jax, jax.numpy as jnp
        import numpy as np
        import math
        B, S, D_IN, D_KQ, D_OUT = (4, 256, 128, 128, 128)
        Q = jnp.einsum('bsd,kd->bsk', x, Wq) + bq
        K = jnp.einsum('bsd,kd->bsk', x, Wk) + bk
        V = jnp.einsum('bsd,od->bso', x, Wv) + bv
        scale = 1.0 / math.sqrt(D_KQ)
        attn = jnp.einsum('bqk,bsk->bqs', Q, K) * scale
        s = attn.shape[-1]
        causal = jnp.tril(jnp.ones((s, s), dtype=bool))
        attn = jnp.where(causal[None, :, :], attn, -jnp.inf)
        attn = jax.nn.softmax(attn, axis=-1)
        Z = jnp.einsum('bqs,bso->bqo', attn, V)
        return Z

    def _L0_ffn_ref(x, expert_sel, keys, values):
        import jax, jax.numpy as jnp
        import numpy as np
        N_HEADS = 4
        B, S, d = x.shape
        n_experts = keys.shape[0]
        xf = x.reshape(-1, d)
        N = xf.shape[0]
        logits = xf @ expert_sel.T
        sel = jax.nn.sigmoid(logits)
        sel_val, sel_idx = jax.lax.top_k(sel, N_HEADS)
        gates = jnp.zeros((N, n_experts), dtype=x.dtype)
        gates = gates.at[jnp.arange(N)[:, None], sel_idx].set(sel_val)
        h = jnp.einsum('nd,kde->nke', xf, keys)
        scores = jax.nn.relu(h) * gates[:, :, None]
        out = jnp.einsum('nke,kev->nv', scores, values)
        return out.reshape(B, S, -1)
    x = L0_attn_x
    x = x + 0.5 * _L0_ffn_ref(_layernorm(x, axis=-1), L0_ffn_expert_sel, L0_ffn_keys, L0_ffn_values)
    x = x + _L0_attn_ref(_layernorm(x, axis=-1), L0_attn_Wq, L0_attn_bq, L0_attn_Wk, L0_attn_bk, L0_attn_Wv, L0_attn_bv)
    x = x + 0.5 * _L0_ffn_ref(_layernorm(x, axis=-1), L0_ffn_expert_sel, L0_ffn_keys, L0_ffn_values)
    return x

_drawn_inputs = setup_inputs


def setup_inputs(seed=0):
    import zlib

    import numpy as np

    out = dict(_drawn_inputs(seed))
    spreads = {}
    factors = {'L0_attn_Wq': 8.0, 'L0_attn_bq': 22.081, 'L0_attn_Wk': 8.0, 'L0_attn_bk': 64.0}
    for name, (base, spread) in spreads.items():
        noise = np.random.default_rng([zlib.crc32(name.encode()), seed]).standard_normal(out[name].shape)
        drawn = base * np.exp(spread * noise) if base else spread * noise
        out[name] = jnp.asarray(drawn.astype(out[name].dtype))
    for name, factor in factors.items():
        out[name] = (out[name] * factor).astype(out[name].dtype)
    return out
```

```python
import concourse.bass as bass
from concourse import mybir
from contextlib import ExitStack
import math


class SelfSync:

    def __init__(self, eng, sem):
        self.eng, self.sem, self.count, self.loop_part = eng, sem, 0, None

    def did(self, instruction):
        instruction.then_inc(self.sem, 1)
        self.count += 1

    def wait(self):
        self.eng.wait_ge(self.sem, self.count if self.loop_part is None else self.loop_part + self.count)


def moe_attention_macaron_kernel(nc, x, Wq, bq, Wk, bk, Wv, bv, expert_sel, keys, values, out):
    fp32, bf16 = mybir.dt.float32, mybir.dt.bfloat16
    i32, u32 = mybir.dt.int32, mybir.dt.uint32
    ALU, ACT, AX = mybir.AluOpType, mybir.ActivationFunctionType, mybir.AxisListType

    P = 128
    B, S, D = x.shape
    E = keys.shape[0]
    TOP = 4
    NT = B * S // P
    HALVES = 2
    HT = NT // HALVES
    ROUTES = 2 * HALVES
    CH = 4
    RC = HT // CH
    BT = S // P
    BC = BT // CH
    SG = 4
    NG = -(-(HT * TOP + E - 1) // SG)
    SLOTS = NG * SG * P
    UN = 4
    EPS = 1e-5
    SCALE = 1.0 / math.sqrt(D)
    NEVER = -3.0e38
    LOGIT_CAP = 17.5

    ROUTE_BASE = [0, RC, 2 * RC + 2 * BC, 3 * RC + 4 * BC]
    ATT_BASE = [2 * RC, 3 * RC + 2 * BC]

    x_t = x.rearrange("b (t p) d -> p (b t) d", p=P)
    out_t = out.rearrange("b (t p) d -> p (b t) d", p=P)

    ctx = ExitStack()
    with ctx:
        def sb(name, shape, dt=fp32):
            return ctx.enter_context(nc.sbuf_tensor(name, shape, dt))

        def pb(name, shape, dt=fp32):
            return ctx.enter_context(nc.psum_tensor(name, shape, dt))

        def sem(name):
            return ctx.enter_context(nc.semaphore(name))

        Xs = [nc.dram_tensor(f"sorted_in_{h}", [SLOTS, D], fp32).ap() for h in range(HALVES)]
        Ys = [nc.dram_tensor(f"sorted_out_{h}", [SLOTS, D], fp32).ap() for h in range(HALVES)]
        Xs_g = [a.rearrange("(g q p) d -> g p q d", q=SG, p=P) for a in Xs]
        Ys_g = [a.rearrange("(g q p) d -> g p q d", q=SG, p=P) for a in Ys]

        res = sb("res", [P, NT, D])
        xln = sb("xln", [P, NT, D])
        keys_sb = sb("keys_sb", [P, E, P])
        vals_sb = sb("vals_sb", [P, E, D])
        xin = sb("xin", [P, UN, SG, D])
        zero = sb("zero", [P, 2048])
        wk = sb("wk", [P, 2, SG, P])
        sxT = sb("sxT", [P, 2, SG * P])
        hT = sb("hT", [P, 2, SG * P])
        yout = sb("yout", [P, 2, SG, D])
        yg = sb("yg", [P, 2, TOP, D])
        ident = sb("ident", [P, P])
        ident_b = sb("ident_b", [P, P], bf16)
        later = sb("later", [P, P], bf16)
        before = sb("before", [P, P], bf16)
        ones_b = sb("ones_b", [P, P], bf16)
        ones_f = sb("ones_f", [E, P])
        upto = sb("upto", [E, E])
        iota_ei = sb("iota_ei", [P, E], i32)
        iota_e = sb("iota_e", [P, E])
        iota_ji = sb("iota_ji", [E, NG * SG], i32)
        iota_j = sb("iota_j", [E, NG * SG])
        restart = sb("restart", [P, E, HT], bf16)
        eps_c = sb("eps_c", [P, 1])
        w_in = sb("w_in", [P, 4, D])
        wT = sb("wT", [P, 4, P])
        bq_c = sb("bq_c", [P, 1])
        bk_c = sb("bk_c", [P, 1])
        bv_r = sb("bv_r", [P, D])
        stats = sb("stats", [P, 2, CH, 6])
        msum, mdif, dev2, mean, mdif2, var = (sb(n, [P, 2, CH]) for n in ("msum", "mdif", "dev2", "mean", "mdif2", "var"))
        lnv = sb("lnv", [P, 2, CH])
        rstd = sb("rstd", [P, 2, CH])
        nT = sb("nT", [P, 2, CH * P])
        lg = sb("lg", [P, HT, E])
        top = sb("top", [P, HT, 8])
        topi = sb("topi", [P, HT, 8], u32)
        topf = sb("topf", [P, HT, TOP])
        hot = sb("hot", [P, TOP, E, HT], bf16)
        pair = sb("pair", [P, 2, E, HT], bf16)
        mask = sb("mask", [P, E, HT], bf16)
        runs = sb("runs", [P, E, HT], bf16)
        prod = sb("prod", [P, E, HT])
        posf = sb("posf", [P, HT, TOP])
        pos = sb("pos", [P, NT, TOP], u32)
        ge = sb("ge", [P, HT, TOP])
        gate = sb("gate", [P, NT, TOP])
        cnt_i = sb("cnt_i", [E, 1], i32)
        cnt_s = sb("cnt_s", [E, 1], i32)
        tiles_f = sb("tiles_f", [E, 1])
        end_c = sb("end_c", [E, 1])
        start_a = sb("start_a", [E, 1])
        start_c = sb("start_c", [E, 1])
        start_d = sb("start_d", [E, E])
        past = sb("past", [E, NG * SG], bf16)
        owner = sb("owner", [1, HALVES, NG * SG], i32)
        xa = sb("xa", [P, BT, D])
        QT = sb("QT", [P, S])
        KT = sb("KT", [P, S])
        V = sb("V", [P, BT, D])
        Pm = sb("Pm", [P, 2, S])
        PT = sb("PT", [P, 2, S])
        nmax = sb("nmax", [P, 2, 1])
        rowsum = sb("rowsum", [P, 2, 1])
        rinv = sb("rinv", [P, 2, 1])

        bank01 = pb("bank01", [P, 2, 512])
        bank23 = pb("bank23", [P, 2, 512])
        bank45 = pb("bank45", [P, 2, 512])
        bank67 = pb("bank67", [P, 2, 512])

        x_in = [sem(f"x_in{c}") for c in range(NT // CH)]
        w_loaded = sem("w_loaded")
        keys_loaded = sem("keys_loaded")
        vals_loaded = sem("vals_loaded")
        filled = [sem(f"filled{h}") for h in range(HALVES)]
        zero_ready = sem("zero_ready")
        const_ready = sem("const_ready")
        pool_self = sem("pool_self")
        w_turned = sem("w_turned")
        w_ready = sem("w_ready")
        stats_ready = sem("stats_ready")
        ln_ready = sem("ln_ready")
        rstd_ready = sem("rstd_ready")
        normed = sem("normed")
        turned = sem("turned")
        nT_ready = sem("nT_ready")
        chunk_mm = sem("chunk_mm")
        logits_out = sem("logits_out")
        gate_in = sem("gate_in")
        gate_exp = sem("gate_exp")
        runs_ready = sem("runs_ready")
        cnt_mm = sem("cnt_mm")
        tiles_ready = sem("tiles_ready")
        end_mm = sem("end_mm")
        start_ready = sem("start_ready")
        owner_mm = sem("owner_mm")
        owner_ready = sem("owner_ready")
        rank_mm = sem("rank_mm")
        pos_ready = sem("pos_ready")
        scattered = [sem(f"scattered{h}") for h in range(HALVES)]
        xin_loaded = [sem(f"xin_loaded{s}") for s in range(UN)]
        slots_turned = sem("slots_turned")
        sxT_ready = sem("sxT_ready")
        keys_staged = sem("keys_staged")
        h_mm = sem("h_mm")
        h_ready = sem("h_ready")
        y_mm = sem("y_mm")
        y_ready = sem("y_ready")
        y_stored = [sem(f"y_stored{s}") for s in range(2)]
        gathered = [sem(f"gathered{s}") for s in range(2)]
        combined = sem("combined")
        q_mm, k_mm = sem("q_mm"), sem("k_mm")
        q_ready, k_ready, v_ready = sem("q_ready"), sem("k_ready"), sem("v_ready")
        s_mm = sem("s_mm")
        max_ready = sem("max_ready")
        exp_ready = sem("exp_ready")
        p_turned = sem("p_turned")
        pT_ready = sem("pT_ready")
        z_mm = sem("z_mm")
        z_added = sem("z_added")
        dve_self = sem("dve_self")
        out_stored = sem("out_stored")

        block = ctx.enter_context(nc.Block())

        def tile_of(buf, t):
            return buf[:, bass.ds(t, 1), :].rearrange("p o d -> p (o d)")

        def skewed(eng, r, step, lo=-2):
            for g in range(lo, 0):
                step(g, r * NG + g, g)
            if r == 0:
                for g in range(UN):
                    step(g, g, g)
            first_turn = 1 if r == 0 else 0
            with eng.Fori(first_turn, NG // UN - 1) as i:
                for u in range(UN):
                    step(None, i * UN + (r * NG + u), u)
            for g in range(NG - UN, NG):
                step(g, r * NG + g, g)

        @block.sync
        def _(sp):
            for c in range(NT // CH):
                if c == 1:
                    sp.dma_start(w_in[:, 0, :], Wq).then_inc(w_loaded, 16)
                    sp.dma_start(w_in[:, 1, :], Wk).then_inc(w_loaded, 16)
                    sp.dma_start(w_in[:, 2, :], Wv).then_inc(w_loaded, 16)
                    sp.dma_start(w_in[0:E, 3, :], expert_sel).then_inc(w_loaded, 16)
                    sp.dma_start(bq_c[:, :], bq.rearrange("(p o) -> p o", o=1)).then_inc(w_loaded, 16)
                    sp.dma_start(bk_c[:, :], bk.rearrange("(p o) -> p o", o=1)).then_inc(w_loaded, 16)
                    sp.dma_start(bv_r[:, :], bv.rearrange("(o d) -> o d", o=1).to_broadcast([P, D])).then_inc(w_loaded, 16)
                sp.dma_start(res[:, c * CH:(c + 1) * CH, :], x_t[:, c * CH:(c + 1) * CH, :]).then_inc(x_in[c], 16)
            sp.wait_ge(zero_ready, 1)
            rows = P * zero.shape[1] // D
            for h in range(HALVES):
                for k in range(SLOTS // rows):
                    sp.dma_start(Xs[h][k * rows:(k + 1) * rows, :].rearrange("(p a) d -> p (a d)", p=P),
                                 zero[:, :]).then_inc(filled[h], 16)
                if h == 0:
                    sp.dma_start(keys_sb[:, :, :], keys.rearrange("k d e -> d k e")).then_inc(keys_loaded, 16)
                    sp.dma_start(vals_sb[:, :, :], values.rearrange("k e v -> e k v")).then_inc(vals_loaded, 16)

            for r in range(ROUTES):
                h = r % HALVES
                n0 = r * NG

                def load(g, n, s):
                    if not isinstance(n, int) or n >= UN:
                        sp.wait_ge(slots_turned, n - (UN - 1))
                    sp.dma_start(xin[:, s, :, :], Xs_g[h][bass.ds(g, 1)].rearrange("o p q d -> (o p) q d")
                                 if not isinstance(g, int) else Xs_g[h][g]).then_inc(xin_loaded[s], 16)

                def store(g, n, s):
                    sp.wait_ge(y_ready, n + 1)
                    sp.dma_start(Ys_g[h][bass.ds(g, 1)].rearrange("o p q d -> (o p) q d")
                                 if not isinstance(g, int) else Ys_g[h][g],
                                 yout[:, s, :, :]).then_inc(y_stored[s], 16)

                sp.wait_ge(scattered[h], 16 * TOP * HT * (r // HALVES + 1))
                if r >= HALVES:
                    sp.wait_ge(combined, HT * (r - HALVES + 1))
                for g in range(UN + 2):
                    load(g, n0 + g, g % UN)
                turns = (NG - UN - 2) // UN
                with sp.Fori(0, turns) as i:
                    for u in range(UN):
                        load(i * UN + (UN + 2 + u), i * UN + (n0 + UN + 2 + u), (2 + u) % UN)
                        store(i * UN + u, i * UN + (n0 + u), u % 2)
                for g in range(turns * UN, NG):
                    if g + UN + 2 < NG:
                        load(g + UN + 2, n0 + g + UN + 2, (g + UN + 2) % UN)
                    store(g, n0 + g, g % 2)

            for c in range(NT // CH):
                sp.wait_ge(combined, NT + (c + 1) * CH)
                sp.dma_start(out_t[:, c * CH:(c + 1) * CH, :], res[:, c * CH:(c + 1) * CH, :]).then_inc(out_stored, 16)
            sp.wait_ge(out_stored, 16 * (NT // CH))

        @block.gpsimd
        def _(gp):
            me = SelfSync(gp, pool_self)
            nc.gpsimd.memset(zero[:, :], 0.0).then_inc(zero_ready, 1)
            me.did(nc.gpsimd.memset(ident[:, :], 0.0))
            me.did(nc.gpsimd.memset(ident_b[:, :], 0.0))
            me.did(nc.gpsimd.memset(later[:, :], 0.0))
            me.did(nc.gpsimd.memset(before[:, :], 0.0))
            me.did(nc.gpsimd.memset(upto[:, :], 1.0))
            me.did(nc.gpsimd.memset(restart[:, :, :], 1.0))
            me.wait()
            for buf, op, fill, step, mult, n in (
                    (ident, ALU.not_equal, 1.0, -1, 1, P), (ident_b, ALU.not_equal, 1.0, -1, 1, P),
                    (later, ALU.is_ge, NEVER, -1, 1, P), (before, ALU.is_gt, -1.0, 1, -1, P),
                    (upto, ALU.is_ge, 0.0, 1, -1, E)):
                nc.gpsimd.affine_select(out=buf[:, :], in_=buf[:, :], compare_op=op, fill=fill, base=0,
                                        pattern=[[step, n]], channel_multiplier=mult).then_inc(const_ready, 1)
            nc.gpsimd.memset(restart[:, :, 0:1], 0.0).then_inc(const_ready, 1)
            nc.gpsimd.memset(ones_b[:, :], 1.0).then_inc(const_ready, 1)
            nc.gpsimd.memset(ones_f[:, :], 1.0).then_inc(const_ready, 1)
            nc.gpsimd.memset(eps_c[:, :], EPS).then_inc(const_ready, 1)
            nc.gpsimd.iota(iota_ei[:, :], pattern=[[1, E]], base=0, channel_multiplier=0).then_inc(const_ready, 1)
            nc.gpsimd.iota(iota_ji[:, :], pattern=[[1, NG * SG]], base=0, channel_multiplier=0).then_inc(const_ready, 1)

            def scatter(r):
                h = r % HALVES
                gp.wait_ge(pos_ready, r + 1)
                if r < HALVES:
                    gp.wait_ge(filled[h], 16 * (SLOTS * D // (P * zero.shape[1])))
                else:
                    gp.wait_ge(slots_turned, NG * (r - HALVES + 1))
                for t in range(h * HT, (h + 1) * HT):
                    for k in range(TOP):
                        nc.gpsimd.indirect_dma_start(
                            out=Xs[h], out_offset=bass.IndirectOffsetOnAxis(ap=pos[:, t, k:k + 1], axis=0),
                            in_=xln[:, t, :], in_offset=None).then_inc(scattered[h], 16)

            def gather(r):
                h = r % HALVES
                for s in range(2):
                    gp.wait_ge(y_stored[s], 16 * (NG // 2) * (r + 1))
                for t in range(HT):
                    m = r * HT + t
                    if m >= 2:
                        gp.wait_ge(combined, m - 1)
                    for k in range(TOP):
                        nc.gpsimd.indirect_dma_start(
                            out=yg[:, m % 2, k, :], out_offset=None, in_=Ys[h],
                            in_offset=bass.IndirectOffsetOnAxis(ap=pos[:, h * HT + t, k:k + 1], axis=0),
                        ).then_inc(gathered[m % 2], 16)

            for f in range(2):
                scatter(2 * f)
                scatter(2 * f + 1)
                gather(2 * f)
                gather(2 * f + 1)

        @block.tensor
        def _(pe):
            pe.wait_ge(const_ready, 11)
            pe.wait_ge(w_loaded, 16 * 7)
            for j in range(4):
                n = P if j < 3 else E
                last = nc.tensor.transpose(bank67[:, 0, j * P:j * P + n], w_in[0:n, j, :], ident[0:n, 0:n])
            last.then_inc(w_turned, 1)

            def turn_chunk(idx, src):
                pe.wait_ge(normed, idx + 1)
                if not isinstance(idx, int) or idx >= 2:
                    pe.wait_ge(nT_ready, idx - 1)
                for q in range(CH):
                    last = nc.tensor.transpose(bank01[:, src[0], q * P:(q + 1) * P], src[1](q), ident[:, :])
                last.then_inc(turned, 1)

            def route(r):
                h = r % HALVES

                def logits(c):
                    idx = ROUTE_BASE[r] + c
                    pe.wait_ge(nT_ready, idx + 1)
                    if r * RC + c >= 2:
                        pe.wait_ge(logits_out, r * RC + c - 1)
                    for q in range(CH):
                        last = nc.tensor.matmul(bank23[:, c % 2, q * E:(q + 1) * E], nT[:, c % 2, q * P:(q + 1) * P],
                                                wT[:, 3, 0:E], start=True, stop=True)
                    last.then_inc(chunk_mm, 1)

                if r == 0:
                    pe.wait_ge(w_ready, 1)
                if r == 2:
                    pe.wait_ge(z_added, 2 * BT)
                if r == 3:
                    pe.wait_ge(z_added, 4 * BT)
                for c in range(RC + 1):
                    if c < RC:
                        t0 = h * HT + c * CH
                        turn_chunk(ROUTE_BASE[r] + c, (c % 2, lambda q, t0=t0: xln[:, t0 + q, :]))
                    if c >= 1:
                        logits(c - 1)
                pe.wait_ge(runs_ready, r + 1)
                nc.tensor.matmul(bank67[0:E, 0, 0:1], runs[:, :, HT - 1], ones_b[:, 0:1],
                                 start=True, stop=True).then_inc(cnt_mm, 1)
                eh = E // 2
                for j in range(2):
                    nc.tensor.matmul(bank45[:, j, :], before[:, :], mask[:, j * eh:(j + 1) * eh, :].rearrange("p e t -> p (e t)"),
                                     start=True, stop=False)
                    nc.tensor.matmul(bank45[:, j, :], ones_b[:, :], runs[:, j * eh:(j + 1) * eh, :].rearrange("p e t -> p (e t)"),
                                     start=False, stop=False)
                pe.wait_ge(tiles_ready, r + 1)
                nc.tensor.matmul(bank67[0:E, 0, 0:1], upto[:, :], tiles_f[:, :], start=True, stop=True).then_inc(end_mm, 1)
                pe.wait_ge(start_ready, r + 1)
                nc.tensor.matmul(bank67[0:1, 1, 0:NG * SG], ones_b[0:E, 0:1], past[:, :],
                                 start=True, stop=True).then_inc(owner_mm, 1)
                for j in range(2):
                    last = nc.tensor.matmul(bank45[:, j, :].rearrange("p (e t) -> p e t", t=HT), ones_f[:, :],
                                            start_d[:, j * eh:(j + 1) * eh].unsqueeze(2).to_broadcast([E, eh, HT]),
                                            start=False, stop=True)
                last.then_inc(rank_mm, 1)

            def experts(r):
                h = r % HALVES
                regs = [pe.alloc_register(f"pe_owner{r}_{q}") for q in range(SG)]
                pe.wait_ge(owner_ready, r + 1)
                pe.wait_ge(pos_ready, r + 1)
                if r == 0:
                    pe.wait_ge(vals_loaded, 16)

                def turn(n, s, u):
                    pe.wait_ge(xin_loaded[u], u_count(n, u))
                    if not isinstance(n, int) or n >= 2:
                        pe.wait_ge(sxT_ready, n - 1)
                    for q in range(SG):
                        last = nc.tensor.transpose(bank01[:, s, q * P:(q + 1) * P], xin[:, u, q, :], ident[:, :])
                    last.then_inc(slots_turned, 1)

                def u_count(n, u):
                    return (n - u) * (16 // UN) + 16 if not isinstance(n, int) else 16 * (n // UN + 1)

                def first(n, s):
                    pe.wait_ge(sxT_ready, n + 1)
                    pe.wait_ge(keys_staged, n + 1)
                    if not isinstance(n, int) or n >= 2:
                        pe.wait_ge(h_ready, n - 1)
                    for q in range(SG):
                        last = nc.tensor.matmul(bank23[:, s, q * P:(q + 1) * P], wk[:, s, q, :],
                                                sxT[:, s, q * P:(q + 1) * P], start=True, stop=True)
                    last.then_inc(h_mm, 1)

                def second(n, s, g):
                    pe.load(regs, owner[0:1, h, bass.ds(g * SG, SG)])
                    pe.wait_ge(h_ready, n + 1)
                    if not isinstance(n, int) or n >= 2:
                        pe.wait_ge(y_ready, n - 1)
                    for q in range(SG):
                        e = pe.snap(regs[q], min_val=0, max_val=E - 1)
                        last = nc.tensor.matmul(bank45[:, s, q * D:(q + 1) * D], hT[:, s, q * P:(q + 1) * P],
                                                vals_sb[:, bass.ds(e, 1), :].rearrange("p o d -> p (o d)"),
                                                start=True, stop=True)
                    last.then_inc(y_mm, 1)

                def step(g, n, u):
                    if g is None or g + 2 < NG:
                        turn(n + 2, u % 2, (u + 2) % UN)
                    if g is None or (g >= -1 and g + 1 < NG):
                        first(n + 1, (u + 1) % 2)
                    if g is None or g >= 0:
                        second(n, u % 2, n - r * NG)

                skewed(pe, r, step)

            def attend(pair):
                with pe.Fori(0, 2) as bl:
                    b = bl + 2 * pair
                    for c in range(BC):
                        idx = bl * BC + (ATT_BASE[pair] + c)
                        turn_chunk(idx, (c % 2, lambda q, c=c: xa[:, c * CH + q, :]))
                        pe.wait_ge(nT_ready, idx + 1)
                        bc = b * BC + c
                        banks = [(3 * c + j) % 2 for j in range(3)]
                        if c:
                            pe.wait_ge(k_ready, bc)
                        nc.tensor.matmul(bank23[:, banks[0], :], wT[:, 0, :], nT[:, c, :],
                                         start=True, stop=True).then_inc(q_mm, 1)
                        if c:
                            pe.wait_ge(v_ready, bc)
                        nc.tensor.matmul(bank23[:, banks[1], :], wT[:, 1, :], nT[:, c, :],
                                         start=True, stop=True).then_inc(k_mm, 1)
                        pe.wait_ge(q_ready, bc + 1)
                        for q in range(CH):
                            last = nc.tensor.matmul(bank23[:, banks[2], q * D:(q + 1) * D], nT[:, c, q * P:(q + 1) * P],
                                                    wT[:, 2, :], start=True, stop=True)
                        last.then_inc(chunk_mm, 1)
                    sc = (bank45, bank67)

                    def scores(i):
                        z = b * BT + i
                        if i == 0:
                            pe.wait_ge(k_ready, b * BC + BC)
                            pe.wait_ge(v_ready, b * BC + BC)
                        if i >= 2:
                            pe.wait_ge(exp_ready, z - 1)
                        w = (i + 1) * P
                        for c in range(-(-w // 512)):
                            n = min(512, w - c * 512)
                            diag = c * 512 + n == w
                            last = nc.tensor.matmul(sc[i % 2][:, c, 0:n], QT[:, i * P:(i + 1) * P],
                                                    KT[:, c * 512:c * 512 + n], start=True, stop=not diag)
                            if diag:
                                last = nc.tensor.matmul(sc[i % 2][:, c, n - P:n], ident_b[:, :], later[:, :],
                                                        start=False, stop=True)
                        last.then_inc(s_mm, 1)

                    def turn_probs(i):
                        z = b * BT + i
                        pe.wait_ge(exp_ready, z + 1)
                        if i >= 1:
                            pe.wait_ge(pT_ready, z)
                        for j in range(i + 1):
                            last = nc.tensor.transpose(bank01[:, j // 4, (j % 4) * P:(j % 4 + 1) * P],
                                                       Pm[:, i % 2, j * P:(j + 1) * P], ident[:, :])
                        last.then_inc(p_turned, 1)

                    def weigh(i):
                        z = b * BT + i
                        pe.wait_ge(pT_ready, z + 1)
                        if i >= 2:
                            pe.wait_ge(z_added, z - 1)
                        for j in range(i + 1):
                            last = nc.tensor.matmul(bank23[:, i % 2, 0:D], PT[:, i % 2, j * P:(j + 1) * P], V[:, j, :],
                                                    start=(j == 0), stop=(j == i))
                        last.then_inc(z_mm, 1)

                    scores(0)
                    for i in range(BT):
                        if i + 1 < BT:
                            scores(i + 1)
                        turn_probs(i)
                        weigh(i)

            route(0)
            route(1)
            experts(0)
            experts(1)
            attend(0)
            route(2)
            attend(1)
            route(3)
            experts(2)
            experts(3)

        @block.scalar
        def _(act):
            nc.scalar.preload_act_table_set("natural_log_exp_and_others")
            act.wait_ge(w_turned, 1)
            nc.scalar.copy(wT[:, 0:3, :], bank67[:, 0, 0:3 * P].rearrange("p (j n) -> p j n", j=3))
            nc.scalar.copy(wT[:, 3, 0:E], bank67[:, 0, 3 * P:3 * P + E]).then_inc(w_ready, 1)

            def inverse_spread(idx, c):
                act.wait_ge(stats_ready, idx + 1)
                nc.scalar.activation(lnv[:, c, :], var[:, c, :], ACT.Ln, bias=eps_c[:, 0:1]).then_inc(ln_ready, 1)
                act.wait_ge(ln_ready, idx + 1)
                nc.scalar.activation(rstd[:, c, :], lnv[:, c, :], ACT.Exp, scale=-0.5).then_inc(rstd_ready, 1)

            def copy_turned(idx, c):
                act.wait_ge(turned, idx + 1)
                if not isinstance(idx, int) or idx >= 2:
                    act.wait_ge(chunk_mm, idx - 1)
                nc.scalar.copy(nT[:, c, :], bank01[:, c, :]).then_inc(nT_ready, 1)

            def route(r):
                for c in range(RC + 1):
                    if c < RC:
                        inverse_spread(ROUTE_BASE[r] + c, c % 2)
                    if c >= 1:
                        copy_turned(ROUTE_BASE[r] + c - 1, (c - 1) % 2)
                act.wait_ge(gate_in, (r + 1) * RC)
                nc.scalar.activation(ge[:, :, :], top[:, :, 0:TOP], ACT.Exp, scale=-1.0).then_inc(gate_exp, 1)

            def experts(r):
                def step(g, n, u):
                    if g is None or g + 2 < NG:
                        m = n + 2
                        act.wait_ge(slots_turned, m + 1)
                        if not isinstance(m, int) or m >= 2:
                            act.wait_ge(h_mm, m - 1)
                        nc.scalar.copy(sxT[:, u % 2, :], bank01[:, u % 2, :]).then_inc(sxT_ready, 1)
                    if g is None or (g >= -1 and g + 1 < NG):
                        m = n + 1
                        act.wait_ge(h_mm, m + 1)
                        if not isinstance(m, int) or m >= 2:
                            act.wait_ge(y_mm, m - 1)
                        nc.scalar.activation(hT[:, (u + 1) % 2, :], bank23[:, (u + 1) % 2, :], ACT.Relu).then_inc(h_ready, 1)

                skewed(act, r, step)

            def attend(pair):
                with act.Fori(0, 2) as bl:
                    b = bl + 2 * pair
                    for c in range(BC):
                        inverse_spread(bl * BC + (ATT_BASE[pair] + c), c)
                    for c in range(BC):
                        copy_turned(bl * BC + (ATT_BASE[pair] + c), c)
                        act.wait_ge(k_mm, b * BC + (c + 1))
                        nc.scalar.activation(KT[:, c * 512:(c + 1) * 512], bank23[:, (3 * c + 1) % 2, :], ACT.Identity,
                                             bias=bk_c[:, 0:1]).then_inc(k_ready, 1)
                    for i in range(BT):
                        z = b * BT + i
                        act.wait_ge(max_ready, z + 1)
                        if i >= 2:
                            act.wait_ge(p_turned, z - 1)
                            act.wait_ge(z_added, z - 1)
                        src = (bank45, bank67)[i % 2][:, :, :].rearrange("p a n -> p (a n)")
                        w = (i + 1) * P
                        nc.scalar.activation(Pm[:, i % 2, 0:w], src[:, 0:w], ACT.Exp, bias=nmax[:, i % 2, :],
                                             accum_out=rowsum[:, i % 2, :]).then_inc(exp_ready, 1)

            route(0)
            route(1)
            experts(0)
            experts(1)
            attend(0)
            route(2)
            attend(1)
            route(3)
            experts(2)
            experts(3)

        @block.vector
        def _(dve):
            me = SelfSync(dve, dve_self)
            dve.wait_ge(const_ready, 11)
            nc.vector.tensor_copy(iota_e[:, :], iota_ei[:, :])
            me.did(nc.vector.tensor_copy(iota_j[:, :], iota_ji[:, :]))
            me.wait()

            def spread(idx, c, tile0):
                for q in range(CH):
                    me.did(nc.vector.bn_stats(stats[:, c, q, :], tile_of(res, tile0 + q)))
                me.wait()
                even, odd = stats[:, c, :, 1], stats[:, c, :, 4]
                me.did(nc.vector.tensor_tensor(msum[:, c, :], even, odd, ALU.add))
                me.did(nc.vector.tensor_tensor(mdif[:, c, :], even, odd, ALU.subtract))
                me.did(nc.vector.tensor_tensor(dev2[:, c, :], stats[:, c, :, 2], stats[:, c, :, 5], ALU.add))
                me.wait()
                me.did(nc.vector.tensor_scalar(mean[:, c, :], msum[:, c, :], 0.5, None, ALU.mult))
                me.did(nc.vector.scalar_tensor_tensor(mdif2[:, c, :], mdif[:, c, :], 0.25, mdif[:, c, :], ALU.mult, ALU.mult))
                me.wait()
                nc.vector.scalar_tensor_tensor(var[:, c, :], dev2[:, c, :], 1.0 / D, mdif2[:, c, :],
                                               ALU.mult, ALU.add).then_inc(stats_ready, 1)

            def normalise(idx, c, tile0, dst):
                dve.wait_ge(rstd_ready, idx + 1)
                for q in range(CH):
                    last = nc.vector.tensor_scalar(dst(q), tile_of(res, tile0 + q), mean[:, c, q:q + 1], rstd[:, c, q:q + 1],
                                                   ALU.subtract, ALU.mult)
                last.then_inc(normed, 1)

            def route(r):
                h = r % HALVES
                if r >= HALVES:
                    dve.wait_ge(scattered[h], 16 * TOP * HT)

                def pick(c):
                    dve.wait_ge(chunk_mm, ROUTE_BASE[r] + c + 1)
                    nc.vector.tensor_scalar(lg[:, c * CH:(c + 1) * CH, :], bank23[:, c % 2, 0:CH * E].rearrange("p (q e) -> p q e", e=E),
                                            LOGIT_CAP, -100.0, ALU.min, ALU.max).then_inc(logits_out, 1)
                    dve.wait_ge(logits_out, r * RC + c + 1)
                    for t in range(c * CH, (c + 1) * CH):
                        last = nc.vector.max(top[:, t, :], lg[:, t, :])
                    last.then_inc(gate_in, 1)
                    dve.wait_ge(gate_in, r * RC + c + 1)
                    for t in range(c * CH, (c + 1) * CH):
                        me.did(nc.vector.max_index(topi[:, t, :], top[:, t, :], lg[:, t, :]))

                for s in range(RC + 3):
                    if s < RC:
                        if r < HALVES:
                            dve.wait_ge(x_in[h * RC + s], 16)
                        spread(ROUTE_BASE[r] + s, s % 2, h * HT + s * CH)
                    if 0 <= s - 1 < RC:
                        t0 = h * HT + (s - 1) * CH
                        normalise(ROUTE_BASE[r] + s - 1, (s - 1) % 2, t0, lambda q, t0=t0: xln[:, t0 + q, :])
                    if 0 <= s - 3 < RC:
                        pick(s - 3)
                me.wait()
                me.did(nc.vector.tensor_copy(topf[:, :, :], topi[:, :, 0:TOP]))
                me.wait()
                for k in range(TOP):
                    me.did(nc.vector.tensor_tensor(hot[:, k, :, :], iota_e[:, :].unsqueeze(2).to_broadcast([P, E, HT]),
                                                   topf[:, :, k].unsqueeze(1).to_broadcast([P, E, HT]), ALU.is_equal))
                me.wait()
                for j in range(2):
                    me.did(nc.vector.tensor_tensor(pair[:, j, :, :], hot[:, 2 * j, :, :], hot[:, 2 * j + 1, :, :], ALU.add))
                me.wait()
                me.did(nc.vector.tensor_tensor(mask[:, :, :], pair[:, 0, :, :], pair[:, 1, :, :], ALU.add))
                me.wait()
                nc.vector.tensor_tensor_scan(runs[:, :, :].rearrange("p e t -> p (e t)"), restart[:, :, :].rearrange("p e t -> p (e t)"),
                                             mask[:, :, :].rearrange("p e t -> p (e t)"), 0.0,
                                             ALU.mult, ALU.add).then_inc(runs_ready, 1)
                dve.wait_ge(cnt_mm, r + 1)
                me.did(nc.vector.tensor_scalar(cnt_i[:, :], bank67[0:E, 0, 0:1], float(P - 1), None, ALU.add))
                me.wait()
                me.did(nc.vector.tensor_scalar(cnt_s[:, :], cnt_i[:, :], P.bit_length() - 1, None, ALU.arith_shift_right))
                me.wait()
                nc.vector.tensor_copy(tiles_f[:, :], cnt_s[:, :]).then_inc(tiles_ready, 1)
                dve.wait_ge(tiles_ready, r + 1)
                dve.wait_ge(end_mm, r + 1)
                me.did(nc.vector.tensor_copy(end_c[:, :], bank67[0:E, 0, 0:1]))
                me.wait()
                me.did(nc.vector.tensor_tensor(start_a[:, :], end_c[:, :], tiles_f[:, :], ALU.subtract))
                me.wait()
                me.did(nc.vector.tensor_scalar(start_c[:, :], start_a[:, :], float(P), None, ALU.mult))
                me.did(nc.vector.tensor_scalar(past[:, :], iota_j[:, :], end_c[:, 0:1], None, ALU.is_ge))
                me.wait()
                nc.vector.tensor_scalar(start_d[:, :], ident[0:E, 0:E], start_c[:, 0:1], None, ALU.mult).then_inc(start_ready, 1)
                dve.wait_ge(owner_mm, r + 1)
                nc.vector.tensor_scalar(owner[0:1, h, :], bank67[0:1, 1, 0:NG * SG], float(E - 1), None, ALU.min).then_inc(owner_ready, 1)
                dve.wait_ge(rank_mm, r + 1)
                for k in range(TOP):
                    me.did(nc.vector.tensor_tensor(prod[:, :, :], bank45[:, :, :].rearrange("p a (e t) -> p (a e) t", t=HT),
                                                   hot[:, k, :, :], ALU.mult))
                    me.wait()
                    me.did(nc.vector.tensor_reduce(posf[:, :, k], prod[:, :, :].rearrange("p e t -> p t e"), AX.X, ALU.add))
                    me.wait()
                nc.vector.tensor_copy(pos[:, h * HT:(h + 1) * HT, :], posf[:, :, :]).then_inc(pos_ready, 1)
                dve.wait_ge(gate_exp, r + 1)
                me.did(nc.vector.tensor_scalar(ge[:, :, :], ge[:, :, :], 1.0, 2.0, ALU.add, ALU.mult))
                me.wait()
                me.did(nc.vector.reciprocal(gate[:, h * HT:(h + 1) * HT, :], ge[:, :, :]))
                me.wait()

            def combine(m, tile, s):
                if isinstance(m, int):
                    dve.wait_ge(gathered[s], 16 * TOP * (m // 2 + 1))
                else:
                    dve.wait_ge(gathered[s], m * (16 * TOP // 2) + (2 - s) * (16 * TOP // 2))
                for k in range(TOP):
                    ins = nc.vector.scalar_tensor_tensor(
                        tile_of(res, tile), yg[:, s, k, :], gate[:, bass.ds(tile, 1), k:k + 1].rearrange("p o d -> p (o d)"),
                        tile_of(res, tile), ALU.mult, ALU.add)
                    if k < TOP - 1:
                        me.did(ins)
                        me.wait()
                    else:
                        ins.then_inc(combined, 1)

            def experts(r):
                h = r % HALVES
                regs = [dve.alloc_register(f"dve_owner{r}_{q}") for q in range(SG)]
                dve.wait_ge(owner_ready, r + 1)
                if r == 0:
                    dve.wait_ge(keys_loaded, 16)

                def stage(n, s, g):
                    dve.load(regs, owner[0:1, h, bass.ds(g * SG, SG)])
                    if not isinstance(n, int) or n >= 2:
                        dve.wait_ge(h_mm, n - 1)
                    for q in range(SG):
                        e = dve.snap(regs[q], min_val=0, max_val=E - 1)
                        last = nc.vector.tensor_copy(wk[:, s, q, :], keys_sb[:, bass.ds(e, 1), :].rearrange("p o d -> p (o d)"))
                    last.then_inc(keys_staged, 1)

                def step(g, n, u):
                    if g is None or g + 2 < NG:
                        stage(n + 2, u % 2, n - r * NG + 2)
                    if g is None or g >= 0:
                        dve.wait_ge(y_mm, n + 1)
                        if isinstance(n, int):
                            if n >= 2:
                                dve.wait_ge(y_stored[u % 2], 16 * (n // 2))
                        else:
                            dve.wait_ge(y_stored[u % 2], n * 8 - 8 * (u % 2))
                        nc.vector.tensor_copy(yout[:, u % 2, :, :].rearrange("p q d -> p (q d)"),
                                              bank45[:, u % 2, :]).then_inc(y_ready, 1)
                        if h == 1 and u % 2 == 1:
                            tile_after(g, n, u)

                def tile_after(g, n, u):
                    if g is not None:
                        t = g // 2
                        combine((r - 1) * HT + t, t, t % 2)
                    else:
                        i2 = loop_turn[0]
                        t = i2 * (UN // 2) + u // 2
                        combine(t + (r - 1) * HT, t, (u // 2) % 2)

                loop_turn = [None]
                for g in range(-2, UN if r == 0 else 0):
                    step(g, r * NG + g, g)
                first_turn = 1 if r == 0 else 0
                turns = NG // UN - 1 - first_turn
                per_turn = (UN // 2) * (TOP - 1) if h == 1 else 0
                n_before = me.count
                with dve.Fori(first_turn, first_turn + turns) as i:
                    loop_turn[0] = i
                    me.loop_part = i * per_turn if per_turn else None
                    for u in range(UN):
                        step(None, i * UN + (r * NG + u), u)
                me.loop_part = None
                assert me.count - n_before == per_turn
                me.count += per_turn * (turns - 1)
                for g in range(NG - UN, NG):
                    step(g, r * NG + g, g)

            def attend(pair):
                if pair == 0:
                    dve.wait_ge(combined, HT)
                per_turn = BC * (CH + 5) + BT * (1 + (TOP - 1) * (pair == 0))
                n_before = me.count
                with dve.Fori(0, 2) as bl:
                    me.loop_part = bl * per_turn
                    b = bl + 2 * pair
                    for c in range(BC):
                        spread(bl * BC + (ATT_BASE[pair] + c), c, b * BT + c * CH)
                    for c in range(BC):
                        normalise(bl * BC + (ATT_BASE[pair] + c), c, b * BT + c * CH, lambda q, c=c: xa[:, c * CH + q, :])
                    for c in range(BC):
                        bc = b * BC + c
                        dve.wait_ge(q_mm, bc + 1)
                        nc.vector.tensor_scalar(QT[:, c * 512:(c + 1) * 512], bank23[:, (3 * c) % 2, :], bq_c[:, 0:1], SCALE,
                                                ALU.add, ALU.mult).then_inc(q_ready, 1)
                        dve.wait_ge(chunk_mm, bl * BC + (ATT_BASE[pair] + c + 1))
                        nc.vector.tensor_tensor(V[:, c * CH:(c + 1) * CH, :], bank23[:, (3 * c + 2) % 2, :].rearrange("p (q d) -> p q d", d=D),
                                                bv_r[:, :].unsqueeze(1).to_broadcast([P, CH, D]), ALU.add).then_inc(v_ready, 1)

                    def largest(i):
                        z = b * BT + i
                        dve.wait_ge(s_mm, z + 1)
                        src = (bank45, bank67)[i % 2][:, :, :].rearrange("p a n -> p (a n)")
                        nc.vector.tensor_reduce(nmax[:, i % 2, :], src[:, 0:(i + 1) * P], AX.X, ALU.max,
                                                negate=True).then_inc(max_ready, 1)

                    largest(0)
                    for i in range(BT):
                        z = b * BT + i
                        if i + 1 < BT:
                            largest(i + 1)
                        dve.wait_ge(p_turned, z + 1)
                        if i >= 2:
                            dve.wait_ge(z_mm, z - 1)
                        nc.vector.tensor_copy(PT[:, i % 2, 0:(i + 1) * P],
                                              bank01[:, :, :].rearrange("p a n -> p (a n)")[:, 0:(i + 1) * P]).then_inc(pT_ready, 1)
                        me.did(nc.vector.reciprocal(rinv[:, i % 2, :], rowsum[:, i % 2, :]))
                        me.wait()
                        dve.wait_ge(z_mm, z + 1)
                        nc.vector.scalar_tensor_tensor(tile_of(res, z), bank23[:, i % 2, 0:D], rinv[:, i % 2, :], tile_of(res, z),
                                                       ALU.mult, ALU.add).then_inc(z_added, 1)
                        if pair == 0:
                            combine(z + HT, z + HT, i % 2)
                me.loop_part = None
                assert me.count - n_before == per_turn, (me.count - n_before, per_turn)
                me.count += per_turn

            route(0)
            route(1)
            experts(0)
            experts(1)
            attend(0)
            dve.wait_ge(z_added, 2 * BT)
            route(2)
            attend(1)
            dve.wait_ge(z_added, 4 * BT)
            route(3)
            experts(2)
            experts(3)
            for t in range(HT):
                combine(3 * HT + t, HT + t, t % 2)


_INS = ['L0_attn_x', 'L0_attn_Wq', 'L0_attn_bq', 'L0_attn_Wk', 'L0_attn_bk', 'L0_attn_Wv', 'L0_attn_bv',
        'L0_ffn_expert_sel', 'L0_ffn_keys', 'L0_ffn_values']


def kernel(**inputs):
    import numpy as _np
    import concourse.bacc as _bacc
    from concourse import mybir as _mybir
    from concourse.bass_utils import run_bass_kernel_spmd as _run

    nc = _bacc.Bacc("TRN2", target_bir_lowering=False, num_devices=1)
    arrays, args = {}, []
    for name in _INS:
        a = _np.ascontiguousarray(inputs[name])
        arrays[f"in_{name}_dram"] = a
        args.append(nc.dram_tensor(f"in_{name}_dram", a.shape, _mybir.dt.from_np(a.dtype), kind="ExternalInput").ap())
    shape = inputs['L0_attn_x'].shape
    out = nc.dram_tensor("out_0_dram", shape, _mybir.dt.float32, kind="ExternalOutput").ap()
    moe_attention_macaron_kernel(nc, *args, out)
    r = _run(nc, [arrays], core_ids=[0])
    return r.results[0]["out_0_dram"]
```

```python
import concourse.bass as bass
from concourse import mybir
from contextlib import ExitStack
import math


class SelfSync:

    def __init__(self, eng, sem):
        self.eng, self.sem, self.count, self.loop_part = eng, sem, 0, None

    def did(self, instruction):
        instruction.then_inc(self.sem, 1)
        self.count += 1

    def wait(self):
        self.eng.wait_ge(self.sem, self.count if self.loop_part is None else self.loop_part + self.count)


def moe_attention_macaron_kernel(nc, x, Wq, bq, Wk, bk, Wv, bv, expert_sel, keys, values, out):
    fp32, bf16 = mybir.dt.float32, mybir.dt.bfloat16
    i32, u32 = mybir.dt.int32, mybir.dt.uint32
    ALU, ACT, AX = mybir.AluOpType, mybir.ActivationFunctionType, mybir.AxisListType

    P = 128
    B, S, D = x.shape
    E = keys.shape[0]
    TOP = 4
    NT = B * S // P
    HALVES = 2
    HT = NT // HALVES
    ROUTES = 2 * HALVES
    CH = 4
    RC = HT // CH
    BT = S // P
    BC = BT // CH
    SG = 4
    NG = -(-(HT * TOP + E - 1) // SG)
    SLOTS = NG * SG * P
    UN = 4
    YR = 8
    LAG = UN // 2
    EPS = 1e-5
    SCALE = 1.0 / math.sqrt(D)
    NEVER = -3.0e38
    LOGIT_CAP = 17.5

    ROUTE_BASE = [0, RC, 2 * RC + 2 * BC, 3 * RC + 4 * BC]
    ATT_BASE = [2 * RC, 3 * RC + 2 * BC]

    x_t = x.rearrange("b (t p) d -> p (b t) d", p=P)
    out_t = out.rearrange("b (t p) d -> p (b t) d", p=P)

    ctx = ExitStack()
    with ctx:
        def sb(name, shape, dt=fp32):
            return ctx.enter_context(nc.sbuf_tensor(name, shape, dt))

        def pb(name, shape, dt=fp32):
            return ctx.enter_context(nc.psum_tensor(name, shape, dt))

        def sem(name):
            return ctx.enter_context(nc.semaphore(name))

        Xs = [nc.dram_tensor(f"sorted_in_{h}", [SLOTS, D], fp32).ap() for h in range(HALVES)]
        Ys = [nc.dram_tensor(f"sorted_out_{h}", [SLOTS, D], fp32).ap() for h in range(HALVES)]
        Xs_g = [a.rearrange("(g q p) d -> g p q d", q=SG, p=P) for a in Xs]
        Ys_g = [a.rearrange("(g q p) d -> g p q d", q=SG, p=P) for a in Ys]

        res = sb("res", [P, NT, D])
        xln = sb("xln", [P, NT, D])
        keys_sb = sb("keys_sb", [P, E, P])
        vals_sb = sb("vals_sb", [P, E, D])
        xin = sb("xin", [P, UN, SG, D])
        wk = sb("wk", [P, UN, SG, P])
        sxT = sb("sxT", [P, 2, SG * P])
        hT = sb("hT", [P, 2, SG * P])
        yout = sb("yout", [P, 2, SG, D])
        yg = sb("yg", [P, YR, TOP, D])
        ident = sb("ident", [P, P])
        ident_b = sb("ident_b", [P, P], bf16)
        later = sb("later", [P, P], bf16)
        before = sb("before", [P, P], bf16)
        ones_b = sb("ones_b", [P, P], bf16)
        tile_rows = sb("tile_rows", [E, P], bf16)
        upto = sb("upto", [E, E], bf16)
        iota_ei = sb("iota_ei", [P, E], i32)
        iota_e = sb("iota_e", [P, E, HT], bf16)
        iota_k = sb("iota_k", [P, TOP])
        iota_ji = sb("iota_ji", [E, NG * SG], i32)
        iota_j = sb("iota_j", [E, NG * SG])
        restart = sb("restart", [P, E, HT], bf16)
        eps_c = sb("eps_c", [P, 1])
        w_in = sb("w_in", [P, 4, D])
        wT = sb("wT", [P, 4, P])
        bq_c = sb("bq_c", [P, 1])
        bq_s = sb("bq_s", [P, 1])
        bk_c = sb("bk_c", [P, 1])
        bv_r = sb("bv_r", [P, D])
        stats = sb("stats", [P, 2, CH, 6])
        msum, mdif, dev2, mean, mdif2, var = (sb(n, [P, 2, CH]) for n in ("msum", "mdif", "dev2", "mean", "mdif2", "var"))
        lnv = sb("lnv", [P, 2, CH])
        shift = sb("shift", [P, 2, CH])
        rstd = sb("rstd", [P, 2, CH])
        nT = sb("nT", [P, 2, CH * P])
        QT = sb("QT", [P, 2, S])
        KT = sb("KT", [P, 2, S])
        V = xin[:, :, :, :].rearrange("p u q d -> p (u q) d").rearrange("p (a b) d -> p a b d", a=2)
        Pm = sb("Pm", [P, 2, S])
        PT = sb("PT", [P, 2, S])
        nmax = sb("nmax", [P, 2, 1])
        rowsum = sb("rowsum", [P, 4, 1])
        rinv = sb("rinv", [P, 2, 1])
        lg = sb("lg", [P, HT, E])
        top = sb("top", [P, HT, 8])
        topi = sb("topi", [P, HT, 8], u32)
        topb = sb("topb", [P, TOP, HT], bf16)
        hot = Pm[:, :, :].rearrange("p a n -> p (a n)").bitcast(bf16).rearrange("p (k e t) -> p k e t", k=TOP, e=E)
        prod = sb("prod", [P, E, HT])
        pair = prod[:, :, :].rearrange("p e t -> p (e t)").bitcast(bf16).rearrange("p (j e t) -> p j e t", j=2, e=E)
        mask = sb("mask", [P, E, HT], bf16)
        runs = sb("runs", [P, E, HT], bf16)
        slot = sb("slot", [P, HT, 8])
        pos = sb("pos", [P, NT, TOP], u32)
        ge = sb("ge", [P, HT, TOP])
        gk = sb("gk", [P, HT, TOP])
        rank = sb("rank", [P, HT, TOP])
        above, placed, gsel = (lg[:, i * HT // 4:(i + 1) * HT // 4, :].rearrange("p u (v a b) -> p (u v) a b", a=TOP, b=TOP)
                               for i in range(3))
        gate = sb("gate", [P, NT, TOP])
        cnt_i = sb("cnt_i", [E, 1], i32)
        cnt_s = sb("cnt_s", [E, 1], i32)
        tiles_b = sb("tiles_b", [E, 1], bf16)
        end_c = sb("end_c", [E, 1])
        start_c = sb("start_c", [E, 1])
        start_d = sb("start_d", [E, E], bf16)
        past = sb("past", [E, NG * SG], bf16)
        owner = sb("owner", [1, HALVES, NG * SG], i32)
        zero = PT[:, :, :].rearrange("p a n -> p (a n)")

        bank01 = pb("bank01", [P, 2, 512])
        bank23 = pb("bank23", [P, 2, 512])
        bank45 = pb("bank45", [P, 2, 512])
        bank67 = pb("bank67", [P, 2, 512])

        x_in = [sem(f"x_in{c}") for c in range(NT // CH)]
        w_loaded = sem("w_loaded")
        keys_loaded = sem("keys_loaded")
        vals_loaded = sem("vals_loaded")
        filled = [sem(f"filled{h}") for h in range(HALVES)]
        zero_ready = sem("zero_ready")
        const_ready = sem("const_ready")
        pool_self = sem("pool_self")
        sel_loaded = sem("sel_loaded")
        sel_turned = sem("sel_turned")
        sel_ready = sem("sel_ready")
        w_turned = sem("w_turned")
        w_ready = sem("w_ready")
        stats_ready = sem("stats_ready")
        ln_ready = sem("ln_ready")
        rstd_ready = sem("rstd_ready")
        shift_ready = sem("shift_ready")
        normed = sem("normed")
        turned = sem("turned")
        nT_ready = sem("nT_ready")
        chunk_mm = sem("chunk_mm")
        logits_out = sem("logits_out")
        top_ready = sem("top_ready")
        gate_exp = sem("gate_exp")
        gates_ready = sem("gates_ready")
        runs_ready = sem("runs_ready")
        cnt_mm = sem("cnt_mm")
        tiles_ready = sem("tiles_ready")
        end_mm = sem("end_mm")
        start_ready = sem("start_ready")
        owner_mm = sem("owner_mm")
        owner_ready = sem("owner_ready")
        rank_mm = sem("rank_mm")
        pos_ready = sem("pos_ready")
        scattered = [sem(f"scattered{h}") for h in range(HALVES)]
        xin_loaded = [sem(f"xin_loaded{s}") for s in range(UN)]
        slots_turned = sem("slots_turned")
        sxT_ready = sem("sxT_ready")
        keys_staged = sem("keys_staged")
        h_mm = sem("h_mm")
        h_ready = sem("h_ready")
        y_mm = sem("y_mm")
        y_ready = sem("y_ready")
        y_stored = [sem(f"y_stored{s}") for s in range(2)]
        gathered = [sem(f"gathered{s}") for s in range(2)]
        combined = sem("combined")
        q_mm, k_mm = sem("q_mm"), sem("k_mm")
        q_ready, k_ready, v_ready = sem("q_ready"), sem("k_ready"), sem("v_ready")
        s_mm = sem("s_mm")
        max_ready = sem("max_ready")
        exp_ready = sem("exp_ready")
        p_turned = sem("p_turned")
        pT_ready = sem("pT_ready")
        z_mm = sem("z_mm")
        z_added = sem("z_added")
        dve_self = sem("dve_self")
        out_stored = sem("out_stored")

        block = ctx.enter_context(nc.Block())

        def tile_of(buf, t):
            return buf[:, bass.ds(t, 1), :].rearrange("p o d -> p (o d)")

        def skewed(eng, r, step, lo=-2):
            for g in range(lo, 0):
                step(g, r * NG + g, g)
            if r == 0:
                for g in range(UN):
                    step(g, g, g)
            first_turn = 1 if r == 0 else 0
            with eng.Fori(first_turn, NG // UN - 1) as i:
                for u in range(UN):
                    step(None, i * UN + (r * NG + u), u)
            for g in range(NG - UN, NG):
                step(g, r * NG + g, g)

        @block.sync
        def _(sp):
            for c in range(NT // CH):
                sp.dma_start(res[:, c * CH:(c + 1) * CH, :], x_t[:, c * CH:(c + 1) * CH, :]).then_inc(x_in[c], 16)
            sp.wait_ge(zero_ready, 1)
            rows = P * zero.shape[1] // D
            for h in range(HALVES):
                for k in range(SLOTS // rows):
                    sp.dma_start(Xs[h][k * rows:(k + 1) * rows, :].rearrange("(p a) d -> p (a d)", p=P),
                                 zero[:, :]).then_inc(filled[h], 16)
                if h == 0:
                    sp.dma_start(keys_sb[:, :, :], keys.rearrange("k d e -> d k e")).then_inc(keys_loaded, 16)
                    sp.dma_start(vals_sb[:, :, :], values.rearrange("k e v -> e k v")).then_inc(vals_loaded, 16)

            for r in range(ROUTES):
                h = r % HALVES
                n0 = r * NG

                def load(g, n, s):
                    if not isinstance(n, int) or n >= UN:
                        sp.wait_ge(slots_turned, n - (UN - 1))
                    sp.dma_start(xin[:, s, :, :], Xs_g[h][bass.ds(g, 1)].rearrange("o p q d -> (o p) q d")
                                 if not isinstance(g, int) else Xs_g[h][g]).then_inc(xin_loaded[s], 16)

                def store(g, n, s):
                    sp.wait_ge(y_ready, n + 1)
                    sp.dma_start(Ys_g[h][bass.ds(g, 1)].rearrange("o p q d -> (o p) q d")
                                 if not isinstance(g, int) else Ys_g[h][g],
                                 yout[:, s, :, :]).then_inc(y_stored[s], 16)

                sp.wait_ge(scattered[h], 16 * TOP * HT * (r // HALVES + 1))
                if r >= HALVES:
                    sp.wait_ge(combined, HT * (r - HALVES + 1))
                    sp.wait_ge(z_added, 2 * BT * (NT // HT))
                for g in range(UN + 2):
                    load(g, n0 + g, g % UN)
                turns = (NG - UN - 2) // UN
                with sp.Fori(0, turns) as i:
                    for u in range(UN):
                        load(i * UN + (UN + 2 + u), i * UN + (n0 + UN + 2 + u), (2 + u) % UN)
                        store(i * UN + u, i * UN + (n0 + u), u % 2)
                for g in range(turns * UN, NG):
                    if g + UN + 2 < NG:
                        load(g + UN + 2, n0 + g + UN + 2, (g + UN + 2) % UN)
                    store(g, n0 + g, g % 2)

            for c in range(NT // CH):
                sp.wait_ge(combined, NT + (c + 1) * CH)
                sp.dma_start(out_t[:, c * CH:(c + 1) * CH, :], res[:, c * CH:(c + 1) * CH, :]).then_inc(out_stored, 16)
            sp.wait_ge(out_stored, 16 * (NT // CH))

        @block.gpsimd
        def _(gp):
            me = SelfSync(gp, pool_self)
            me.did(nc.gpsimd.memset(ident[:, :], 0.0))
            me.did(nc.gpsimd.memset(ident_b[:, :], 0.0))
            me.did(nc.gpsimd.memset(later[:, :], 0.0))
            me.did(nc.gpsimd.memset(before[:, :], 0.0))
            me.did(nc.gpsimd.memset(upto[:, :], 1.0))
            me.did(nc.gpsimd.memset(restart[:, :, :], 1.0))
            me.wait()
            for buf, op, fill, step, mult, n in (
                    (ident, ALU.not_equal, 1.0, -1, 1, P), (ident_b, ALU.not_equal, 1.0, -1, 1, P),
                    (later, ALU.is_ge, NEVER, -1, 1, P), (before, ALU.is_gt, -1.0, 1, -1, P),
                    (upto, ALU.is_ge, 0.0, 1, -1, E)):
                nc.gpsimd.affine_select(out=buf[:, :], in_=buf[:, :], compare_op=op, fill=fill, base=0,
                                        pattern=[[step, n]], channel_multiplier=mult).then_inc(const_ready, 1)
            nc.gpsimd.memset(restart[:, :, 0:1], 0.0).then_inc(const_ready, 1)
            nc.gpsimd.memset(ones_b[:, :], 1.0).then_inc(const_ready, 1)
            nc.gpsimd.memset(tile_rows[:, :], float(P)).then_inc(const_ready, 1)
            nc.gpsimd.memset(eps_c[:, :], EPS).then_inc(const_ready, 1)
            nc.gpsimd.iota(iota_ei[:, :], pattern=[[1, E]], base=0, channel_multiplier=0).then_inc(const_ready, 1)
            nc.gpsimd.iota(iota_ji[:, :], pattern=[[1, NG * SG]], base=0, channel_multiplier=0).then_inc(const_ready, 1)

            def scatter(r):
                h = r % HALVES
                if r < HALVES:
                    gp.wait_ge(filled[h], 16 * (SLOTS * D // (P * zero.shape[1])))
                else:
                    gp.wait_ge(slots_turned, NG * (r - HALVES + 1))
                for t in range(h * HT, (h + 1) * HT):
                    if t % CH == 0:
                        gp.wait_ge(pos_ready, r * RC + t % HT // CH + 1)
                    for k in range(TOP):
                        nc.gpsimd.indirect_dma_start(
                            out=Xs[h], out_offset=bass.IndirectOffsetOnAxis(ap=pos[:, t, k:k + 1], axis=0),
                            in_=xln[:, t, :], in_offset=None).then_inc(scattered[h], 16)

            def gather(r):
                h = r % HALVES
                for s in range(2):
                    gp.wait_ge(y_stored[s], 16 * (NG // 2) * (r + 1))
                for t in range(HT):
                    m = r * HT + t
                    if m >= 2:
                        gp.wait_ge(gathered[m % 2], 16 * TOP * (m // 2))
                    if m >= YR:
                        gp.wait_ge(combined, m - YR + 1)
                    for k in range(TOP):
                        nc.gpsimd.indirect_dma_start(
                            out=yg[:, m % YR, k, :], out_offset=None, in_=Ys[h],
                            in_offset=bass.IndirectOffsetOnAxis(ap=pos[:, h * HT + t, k:k + 1], axis=0),
                        ).then_inc(gathered[m % 2], 16)

            for f in range(2):
                scatter(2 * f)
                scatter(2 * f + 1)
                gather(2 * f)
                gather(2 * f + 1)

        @block.tensor
        def _(pe):
            def turn_sel():
                pe.wait_ge(sel_loaded, 16)
                nc.tensor.transpose(bank67[:, 0, 0:E], w_in[0:E, 3, :], ident[0:E, 0:E]).then_inc(sel_turned, 1)

            def turn_weights():
                pe.wait_ge(w_loaded, 16 * 6)
                pe.wait_ge(owner_ready, 1)
                for j in range(3):
                    last = nc.tensor.transpose(bank67[:, 0, j * P:(j + 1) * P], w_in[:, j, :], ident[:, :])
                last.then_inc(w_turned, 1)

            def turn_chunk(idx, s, tile0):
                pe.wait_ge(normed, idx + 1)
                if idx >= 2:
                    pe.wait_ge(nT_ready, idx - 1)
                for q in range(CH):
                    last = nc.tensor.transpose(bank01[:, s, q * P:(q + 1) * P], xln[:, tile0 + q, :], ident[:, :])
                last.then_inc(turned, 1)

            def route(r):
                h = r % HALVES

                def logits(c):
                    idx = ROUTE_BASE[r] + c
                    pe.wait_ge(nT_ready, idx + 1)
                    if r * RC + c >= 2:
                        pe.wait_ge(logits_out, r * RC + c - 1)
                    for q in range(CH):
                        last = nc.tensor.matmul(bank23[:, c % 2, q * E:(q + 1) * E], nT[:, c % 2, q * P:(q + 1) * P],
                                                wT[:, 3, 0:E], start=True, stop=True)
                    last.then_inc(chunk_mm, 1)

                if r == 0:
                    pe.wait_ge(const_ready, 11)
                if r >= HALVES:
                    pe.wait_ge(z_added, 2 * BT * (r - 1))
                for c in range(RC + 1):
                    if c < RC:
                        t0 = h * HT + c * CH
                        turn_chunk(ROUTE_BASE[r] + c, c % 2, t0)
                    if r == 0 and c == 0:
                        turn_sel()
                        pe.wait_ge(sel_ready, 1)
                    if c >= 1:
                        logits(c - 1)
                if r == 1:
                    pe.wait_ge(w_ready, 1)
                pe.wait_ge(runs_ready, r + 1)
                nc.tensor.matmul(bank67[0:E, 0, 0:1], runs[:, :, HT - 1], ones_b[:, 0:1],
                                 start=True, stop=True).then_inc(cnt_mm, 1)
                eh = E // 2
                for j in range(2):
                    nc.tensor.matmul(bank45[:, j, :], before[:, :], mask[:, j * eh:(j + 1) * eh, :].rearrange("p e t -> p (e t)"),
                                     start=True, stop=False)
                    nc.tensor.matmul(bank45[:, j, :], ones_b[:, :], runs[:, j * eh:(j + 1) * eh, :].rearrange("p e t -> p (e t)"),
                                     start=False, stop=False)
                pe.wait_ge(tiles_ready, r + 1)
                nc.tensor.matmul(bank67[0:E, 0, 0:1], upto[:, :], tiles_b[:, :], start=True, stop=True).then_inc(end_mm, 1)
                pe.wait_ge(start_ready, r + 1)
                nc.tensor.matmul(bank67[0:1, 1, 0:NG * SG], ones_b[0:E, 0:1], past[:, :],
                                 start=True, stop=True).then_inc(owner_mm, 1)
                for j in range(2):
                    last = nc.tensor.matmul(bank45[:, j, :].rearrange("p (e t) -> p e t", t=HT), tile_rows[:, :],
                                            start_d[:, j * eh:(j + 1) * eh].unsqueeze(2).to_broadcast([E, eh, HT]),
                                            start=False, stop=True)
                last.then_inc(rank_mm, 1)

            def experts(r):
                h = r % HALVES
                regs = [pe.alloc_register(f"pe_owner{r}_{q}") for q in range(SG)]
                pe.wait_ge(owner_ready, r + 1)
                pe.wait_ge(pos_ready, (r + 1) * RC)
                if r == 0:
                    pe.wait_ge(vals_loaded, 16)

                def turn(n, s, u):
                    pe.wait_ge(xin_loaded[u], u_count(n, u))
                    if not isinstance(n, int) or n >= 2:
                        pe.wait_ge(sxT_ready, n - 1)
                    for q in range(SG):
                        last = nc.tensor.transpose(bank01[:, s, q * P:(q + 1) * P], xin[:, u, q, :], ident[:, :])
                    last.then_inc(slots_turned, 1)

                def u_count(n, u):
                    return (n - u) * (16 // UN) + 16 if not isinstance(n, int) else 16 * (n // UN + 1)

                def first(n, s, u):
                    pe.wait_ge(sxT_ready, n + 1)
                    pe.wait_ge(keys_staged, n + 1)
                    if not isinstance(n, int) or n >= 2:
                        pe.wait_ge(h_ready, n - 1)
                    for q in range(SG):
                        last = nc.tensor.matmul(bank23[:, s, q * P:(q + 1) * P], wk[:, u, q, :],
                                                sxT[:, s, q * P:(q + 1) * P], start=True, stop=True)
                    last.then_inc(h_mm, 1)

                def second(n, s, g):
                    pe.load(regs, owner[0:1, h, bass.ds(g * SG, SG)])
                    pe.wait_ge(h_ready, n + 1)
                    if not isinstance(n, int) or n >= 2:
                        pe.wait_ge(y_ready, n - 1)
                    for q in range(SG):
                        e = pe.snap(regs[q], min_val=0, max_val=E - 1)
                        last = nc.tensor.matmul(bank45[:, s, q * D:(q + 1) * D], hT[:, s, q * P:(q + 1) * P],
                                                vals_sb[:, bass.ds(e, 1), :].rearrange("p o d -> p (o d)"),
                                                start=True, stop=True)
                    last.then_inc(y_mm, 1)

                def step(g, n, u):
                    if g is None or g + 2 < NG:
                        turn(n + 2, u % 2, (u + 2) % UN)
                    if g is None or (g >= -1 and g + 1 < NG):
                        first(n + 1, (u + 1) % 2, (u + 1) % UN)
                    if g is None or g >= 0:
                        second(n, u % 2, n - r * NG)

                skewed(pe, r, step)

            def attend(pair):
                base = ATT_BASE[pair]
                place = ((bank45[:, 0, :], bank45[:, 1, :], bank67[:, 0, :]),
                         (bank67[:, 1, :], bank23[:, 0, :], bank23[:, 1, :]))

                def project(c):
                    n = 2 * BC * pair + c
                    pe.wait_ge(nT_ready, base + c + 1)
                    if c >= 2:
                        pe.wait_ge(q_ready, n - 1)
                        pe.wait_ge(k_ready, n - 1)
                        pe.wait_ge(v_ready, n - 1)
                    to_q, to_k, to_v = place[c % 2]
                    nc.tensor.matmul(to_q, wT[:, 0, :], nT[:, c % 2, :], start=True, stop=True).then_inc(q_mm, 1)
                    nc.tensor.matmul(to_k, wT[:, 1, :], nT[:, c % 2, :], start=True, stop=True).then_inc(k_mm, 1)
                    for q in range(CH):
                        last = nc.tensor.matmul(to_v[:, q * D:(q + 1) * D], nT[:, c % 2, q * P:(q + 1) * P],
                                                wT[:, 2, :], start=True, stop=True)
                    last.then_inc(chunk_mm, 1)

                for c in range(2 * BC + 1):
                    if c < 2 * BC:
                        turn_chunk(base + c, c % 2, pair * HT + c * CH)
                    if c >= 1:
                        project(c - 1)

                score_bank = (bank45, bank67)

                def scores(j):
                    z, row, i = pair * 2 * BT + j, j // BT, j % BT
                    if j == 0:
                        pe.wait_ge(q_ready, 2 * BC * (pair + 1))
                        pe.wait_ge(k_ready, 2 * BC * (pair + 1))
                        pe.wait_ge(v_ready, 2 * BC * (pair + 1))
                    if j >= 2:
                        pe.wait_ge(exp_ready, z - 1)
                    w = (i + 1) * P
                    for c in range(-(-w // 512)):
                        n = min(512, w - c * 512)
                        diag = c * 512 + n == w
                        last = nc.tensor.matmul(score_bank[j % 2][:, c, 0:n], QT[:, row, i * P:(i + 1) * P],
                                                KT[:, row, c * 512:c * 512 + n], start=True, stop=not diag)
                        if diag:
                            last = nc.tensor.matmul(score_bank[j % 2][:, c, n - P:n], ident_b[:, :], later[:, :],
                                                    start=False, stop=True)
                    last.then_inc(s_mm, 1)

                def turn_probs(j):
                    z, i = pair * 2 * BT + j, j % BT
                    pe.wait_ge(exp_ready, z + 1)
                    if z >= 1:
                        pe.wait_ge(pT_ready, z)
                    for n in range(i + 1):
                        last = nc.tensor.transpose(bank01[:, n // 4, (n % 4) * P:(n % 4 + 1) * P],
                                                   Pm[:, j % 2, n * P:(n + 1) * P], ident[:, :])
                    last.then_inc(p_turned, 1)

                def weigh(j):
                    z, row, i = pair * 2 * BT + j, j // BT, j % BT
                    pe.wait_ge(pT_ready, z + 1)
                    if z >= 2:
                        pe.wait_ge(z_added, z - 1)
                    for n in range(i + 1):
                        last = nc.tensor.matmul(bank23[:, j % 2, 0:D], PT[:, j % 2, n * P:(n + 1) * P], V[:, row, n, :],
                                                start=(n == 0), stop=(n == i))
                    last.then_inc(z_mm, 1)

                scores(0)
                scores(1)
                turn_probs(0)
                for j in range(2 * BT):
                    if j + 2 < 2 * BT:
                        scores(j + 2)
                    if j + 1 < 2 * BT:
                        turn_probs(j + 1)
                    weigh(j)

            route(0)
            turn_weights()
            route(1)
            experts(0)
            experts(1)
            attend(0)
            route(2)
            attend(1)
            route(3)
            experts(2)
            experts(3)

        @block.scalar
        def _(act):
            nc.scalar.preload_act_table_set("natural_log_exp_and_others")
            act.dma_start(w_in[0:E, 3, :], expert_sel).then_inc(sel_loaded, 16)
            for j, w in enumerate((Wq, Wk, Wv)):
                act.dma_start(w_in[:, j, :], w).then_inc(w_loaded, 16)
            act.dma_start(bq_c[:, :], bq.rearrange("(p o) -> p o", o=1)).then_inc(w_loaded, 16)
            act.dma_start(bk_c[:, :], bk.rearrange("(p o) -> p o", o=1)).then_inc(w_loaded, 16)
            act.dma_start(bv_r[:, :], bv.rearrange("(o d) -> o d", o=1).to_broadcast([P, D])).then_inc(w_loaded, 16)
            act.wait_ge(const_ready, 11)

            def sel_out():
                act.wait_ge(sel_turned, 1)
                nc.scalar.copy(wT[:, 3, 0:E], bank67[:, 0, 0:E]).then_inc(sel_ready, 1)

            def weights_out():
                act.wait_ge(w_loaded, 16 * 6)
                nc.scalar.mul(bq_s[:, :], bq_c[:, :], SCALE)
                act.wait_ge(w_turned, 1)
                nc.scalar.copy(wT[:, 0:3, :], bank67[:, 0, 0:3 * P].rearrange("p (j n) -> p j n", j=3)).then_inc(w_ready, 1)

            def inverse_spread(idx, c):
                act.wait_ge(stats_ready, idx + 1)
                nc.scalar.activation(lnv[:, c, :], var[:, c, :], ACT.Ln, bias=eps_c[:, 0:1]).then_inc(ln_ready, 1)
                act.wait_ge(ln_ready, idx + 1)
                nc.scalar.activation(rstd[:, c, :], lnv[:, c, :], ACT.Exp, scale=-0.5).then_inc(rstd_ready, 1)

            def normalise(idx, c, tile0):
                act.wait_ge(shift_ready, idx + 1)
                for q in range(CH):
                    last = nc.scalar.activation(xln[:, tile0 + q, :], res[:, tile0 + q, :], ACT.Identity,
                                                bias=shift[:, c, q:q + 1], scale=rstd[:, c, q:q + 1])
                last.then_inc(normed, 1)

            def copy_turned(idx, c):
                act.wait_ge(turned, idx + 1)
                if idx >= 2:
                    act.wait_ge(chunk_mm, idx - 1)
                nc.scalar.copy(nT[:, c, :], bank01[:, c, :]).then_inc(nT_ready, 1)

            def norm_steps(base, chunks, tile0, after=None, once=None):
                for c in range(chunks + 2):
                    if c < chunks:
                        inverse_spread(base + c, c % 2)
                    if 0 <= c - 1 < chunks:
                        normalise(base + c - 1, (c - 1) % 2, tile0 + (c - 1) * CH)
                    if c == 1 and once is not None:
                        once()
                    if 0 <= c - 2:
                        copy_turned(base + c - 2, (c - 2) % 2)
                        if after is not None:
                            after(c - 2)

            def route(r):
                h = r % HALVES
                if r >= HALVES:
                    act.wait_ge(scattered[h], 16 * TOP * HT)
                norm_steps(ROUTE_BASE[r], RC, h * HT, once=sel_out if r == 0 else None)
                act.wait_ge(top_ready, (r + 1) * RC)
                if r >= 1:
                    act.wait_ge(gates_ready, r)
                nc.scalar.activation(ge[:, :, :], top[:, :, 0:TOP], ACT.Exp, scale=-1.0).then_inc(gate_exp, 1)

            def experts(r):
                def step(g, n, u):
                    if g is None or g + 2 < NG:
                        m = n + 2
                        act.wait_ge(slots_turned, m + 1)
                        if not isinstance(m, int) or m >= 2:
                            act.wait_ge(h_mm, m - 1)
                        nc.scalar.copy(sxT[:, u % 2, :], bank01[:, u % 2, :]).then_inc(sxT_ready, 1)
                    if g is None or (g >= -1 and g + 1 < NG):
                        m = n + 1
                        act.wait_ge(h_mm, m + 1)
                        if not isinstance(m, int) or m >= 2:
                            act.wait_ge(y_mm, m - 1)
                        nc.scalar.activation(hT[:, (u + 1) % 2, :], bank23[:, (u + 1) % 2, :], ACT.Relu).then_inc(h_ready, 1)
                    if g is None or g >= 0:
                        act.wait_ge(y_mm, n + 1)
                        if not isinstance(n, int):
                            act.wait_ge(y_stored[u % 2], n * 8 - 8 * (u % 2))
                        elif n >= 2:
                            act.wait_ge(y_stored[u % 2], 16 * (n // 2))
                        nc.scalar.copy(yout[:, u % 2, :, :].rearrange("p q d -> p (q d)"), bank45[:, u % 2, :]).then_inc(y_ready, 1)

                skewed(act, r, step)

            def attend(pair):
                score_bank = (bank45, bank67)
                place = ((bank45[:, 0, :], bank45[:, 1, :]), (bank67[:, 1, :], bank23[:, 0, :]))

                def project_out(c):
                    n = 2 * BC * pair + c
                    row, half = c // BC, c % BC
                    to_q, to_k = place[c % 2]
                    act.wait_ge(q_mm, n + 1)
                    nc.scalar.activation(QT[:, row, half * 512:(half + 1) * 512], to_q, ACT.Identity,
                                         bias=bq_s[:, 0:1], scale=SCALE).then_inc(q_ready, 1)
                    act.wait_ge(k_mm, n + 1)
                    nc.scalar.activation(KT[:, row, half * 512:(half + 1) * 512], to_k, ACT.Identity,
                                         bias=bk_c[:, 0:1]).then_inc(k_ready, 1)

                act.wait_ge(scattered[pair], 16 * TOP * HT)
                norm_steps(ATT_BASE[pair], 2 * BC, pair * HT, lambda c: project_out(c - 1) if c else None)
                project_out(2 * BC - 1)

                def exps(j):
                    z, i = pair * 2 * BT + j, j % BT
                    act.wait_ge(max_ready, z + 1)
                    if z >= 2:
                        act.wait_ge(p_turned, z - 1)
                    if z >= 4:
                        act.wait_ge(z_added, z - 3)
                    w = (i + 1) * P
                    nc.scalar.activation(Pm[:, j % 2, 0:w], score_bank[j % 2][:, :, :].rearrange("p a n -> p (a n)")[:, 0:w],
                                         ACT.Exp, bias=nmax[:, j % 2, :], accum_out=rowsum[:, j % 4, :]).then_inc(exp_ready, 1)

                def probs_out(j):
                    z, i = pair * 2 * BT + j, j % BT
                    act.wait_ge(p_turned, z + 1)
                    if z >= 2:
                        act.wait_ge(z_mm, z - 1)
                    if z == 0:
                        act.wait_ge(filled[HALVES - 1], 16 * (SLOTS * D // (P * zero.shape[1])))
                    w = (i + 1) * P
                    nc.scalar.copy(PT[:, j % 2, 0:w], bank01[:, :, :].rearrange("p a n -> p (a n)")[:, 0:w]).then_inc(pT_ready, 1)

                exps(0)
                exps(1)
                probs_out(0)
                for j in range(2 * BT):
                    if j + 1 < 2 * BT:
                        probs_out(j + 1)
                    if j + 2 < 2 * BT:
                        exps(j + 2)

            route(0)
            weights_out()
            route(1)
            experts(0)
            experts(1)
            attend(0)
            route(2)
            attend(1)
            route(3)
            experts(2)
            experts(3)

        @block.vector
        def _(dve):
            me = SelfSync(dve, dve_self)
            nc.vector.memset(zero, 0.0).then_inc(zero_ready, 1)

            def spread(idx, c, tile0):
                for q in range(CH):
                    me.did(nc.vector.bn_stats(stats[:, c, q, :], res[:, tile0 + q, :]))
                me.wait()
                even, odd = stats[:, c, :, 1], stats[:, c, :, 4]
                me.did(nc.vector.tensor_tensor(msum[:, c, :], even, odd, ALU.add))
                me.did(nc.vector.tensor_tensor(mdif[:, c, :], even, odd, ALU.subtract))
                me.did(nc.vector.tensor_tensor(dev2[:, c, :], stats[:, c, :, 2], stats[:, c, :, 5], ALU.add))
                me.wait()
                me.did(nc.vector.tensor_scalar(mean[:, c, :], msum[:, c, :], -0.5, None, ALU.mult))
                me.did(nc.vector.scalar_tensor_tensor(mdif2[:, c, :], mdif[:, c, :], 0.25, mdif[:, c, :], ALU.mult, ALU.mult))
                me.wait()
                nc.vector.scalar_tensor_tensor(var[:, c, :], dev2[:, c, :], 1.0 / D, mdif2[:, c, :],
                                               ALU.mult, ALU.add).then_inc(stats_ready, 1)

            def shifts(idx, c):
                dve.wait_ge(rstd_ready, idx + 1)
                nc.vector.tensor_tensor(shift[:, c, :], mean[:, c, :], rstd[:, c, :], ALU.mult).then_inc(shift_ready, 1)

            def route(r, between=lambda: None):
                h = r % HALVES

                def pick(c):
                    dve.wait_ge(chunk_mm, ROUTE_BASE[r] + c + 1)
                    nc.vector.tensor_scalar(lg[:, c * CH:(c + 1) * CH, :], bank23[:, c % 2, 0:CH * E].rearrange("p (q e) -> p q e", e=E),
                                            LOGIT_CAP, -100.0, ALU.min, ALU.max).then_inc(logits_out, 1)
                    dve.wait_ge(logits_out, r * RC + c + 1)
                    for t in range(c * CH, (c + 1) * CH):
                        last = nc.vector.max(top[:, t, :], lg[:, t, :])
                    last.then_inc(top_ready, 1)
                    dve.wait_ge(top_ready, r * RC + c + 1)
                    for t in range(c * CH, (c + 1) * CH):
                        me.did(nc.vector.max_index(topi[:, t, :], top[:, t, :], lg[:, t, :]))

                for s in range(RC + 4):
                    if s < RC:
                        if r < HALVES:
                            dve.wait_ge(x_in[h * RC + s], 16)
                        spread(ROUTE_BASE[r] + s, s % 2, h * HT + s * CH)
                    if 0 <= s - 1 < RC:
                        shifts(ROUTE_BASE[r] + s - 1, (s - 1) % 2)
                    if r == 0 and s == RC:
                        dve.wait_ge(const_ready, 11)
                        nc.vector.tensor_copy(iota_e[:, :, :], iota_ei[:, :].unsqueeze(2).to_broadcast([P, E, HT]))
                        nc.vector.tensor_copy(iota_k[:, :], iota_ei[:, 0:TOP])
                        me.did(nc.vector.tensor_copy(iota_j[:, :], iota_ji[:, :]))
                    if s >= 4:
                        pick(s - 4)
                        between()
                me.wait()
                me.did(nc.vector.tensor_copy(topb[:, :, :], topi[:, :, 0:TOP].rearrange("p t k -> p k t")))
                me.wait()
                me.did(nc.vector.tensor_tensor(hot, iota_e[:, :, :].unsqueeze(1).to_broadcast([P, TOP, E, HT]),
                                               topb[:, :, :].unsqueeze(2).to_broadcast([P, TOP, E, HT]), ALU.is_equal))
                me.wait()
                me.did(nc.vector.tensor_tensor(pair, hot[:, 0:2, :, :], hot[:, 2:4, :, :], ALU.add))
                me.wait()
                me.did(nc.vector.tensor_tensor(mask[:, :, :], pair[:, 0, :, :], pair[:, 1, :, :], ALU.add))
                me.wait()
                nc.vector.tensor_tensor_scan(runs[:, :, :].rearrange("p e t -> p (e t)"), restart[:, :, :].rearrange("p e t -> p (e t)"),
                                             mask[:, :, :].rearrange("p e t -> p (e t)"), 0.0,
                                             ALU.mult, ALU.add).then_inc(runs_ready, 1)
                dve.wait_ge(cnt_mm, r + 1)
                me.did(nc.vector.tensor_scalar(cnt_i[:, :], bank67[0:E, 0, 0:1], float(P - 1), None, ALU.add))
                me.wait()
                me.did(nc.vector.tensor_scalar(cnt_s[:, :], cnt_i[:, :], P.bit_length() - 1, None, ALU.arith_shift_right))
                me.wait()
                nc.vector.tensor_copy(tiles_b[:, :], cnt_s[:, :]).then_inc(tiles_ready, 1)
                dve.wait_ge(tiles_ready, r + 1)
                dve.wait_ge(end_mm, r + 1)
                me.did(nc.vector.tensor_copy(end_c[:, :], bank67[0:E, 0, 0:1]))
                me.wait()
                me.did(nc.vector.tensor_tensor(start_c[:, :], end_c[:, :], tiles_b[:, :], ALU.subtract))
                me.did(nc.vector.tensor_scalar(past[:, :], iota_j[:, :], end_c[:, 0:1], None, ALU.is_ge))
                me.wait()
                nc.vector.tensor_scalar(start_d[:, :], ident[0:E, 0:E], start_c[:, 0:1], None, ALU.mult).then_inc(start_ready, 1)
                dve.wait_ge(owner_mm, r + 1)
                nc.vector.tensor_scalar(owner[0:1, h, :], bank67[0:1, 1, 0:NG * SG], float(E - 1), None, ALU.min).then_inc(owner_ready, 1)
                dve.wait_ge(rank_mm, r + 1)
                for c in range(RC):
                    ts = slice(c * CH, (c + 1) * CH)
                    me.did(nc.vector.scalar_tensor_tensor(prod[:, :, ts], bank45[:, :, :].rearrange("p a (e t) -> p (a e) t", t=HT)[:, :, ts],
                                                          1.0, mask[:, :, ts], ALU.add, ALU.mult))
                    me.wait()
                    for t in range(c * CH, (c + 1) * CH):
                        me.did(nc.vector.max(slot[:, t, :], prod[:, :, t]))
                    me.wait()
                    nc.vector.tensor_scalar(pos[:, h * HT + c * CH:h * HT + (c + 1) * CH, :], slot[:, ts, 0:TOP], 1.0, None,
                                            ALU.subtract).then_inc(pos_ready, 1)
                dve.wait_ge(gate_exp, r + 1)
                me.did(nc.vector.tensor_scalar(ge[:, :, :], ge[:, :, :], 1.0, 2.0, ALU.add, ALU.mult))
                full = [P, HT, TOP, TOP]
                me.did(nc.vector.tensor_tensor(above[:, :, :, :], topi[:, :, 0:TOP].unsqueeze(2).to_broadcast(full),
                                               topi[:, :, 0:TOP].unsqueeze(3).to_broadcast(full), ALU.is_gt))
                me.wait()
                me.did(nc.vector.reciprocal(gk[:, :, :], ge[:, :, :]))
                me.did(nc.vector.tensor_reduce(rank[:, :, :], above[:, :, :, :], AX.X, ALU.add))
                me.wait()
                me.did(nc.vector.tensor_tensor(placed[:, :, :, :], rank[:, :, :].unsqueeze(2).to_broadcast(full),
                                               iota_k[:, :].unsqueeze(1).unsqueeze(3).to_broadcast(full), ALU.is_equal))
                me.wait()
                me.did(nc.vector.tensor_tensor(gsel[:, :, :, :], placed[:, :, :, :], gk[:, :, :].unsqueeze(2).to_broadcast(full),
                                               ALU.mult))
                me.wait()
                nc.vector.tensor_reduce(gate[:, h * HT:(h + 1) * HT, :], gsel[:, :, :, :], AX.X, ALU.add).then_inc(gates_ready, 1)
                dve.wait_ge(gates_ready, r + 1)

            def combine(m, tile, s, ring=None):
                if isinstance(m, int):
                    dve.wait_ge(gathered[s], 16 * TOP * (m // 2 + 1))
                    rows = yg[:, m % YR, :, :]
                else:
                    dve.wait_ge(gathered[s], m * (16 * TOP // 2) + (2 - s) * (16 * TOP // 2))
                    rows = yg[:, bass.ds(ring, 1), :, :].rearrange("p o k d -> p (o k) d")
                for k in range(TOP):
                    ins = nc.vector.scalar_tensor_tensor(
                        tile_of(res, tile), rows[:, k, :], gate[:, bass.ds(tile, 1), k:k + 1].rearrange("p o d -> p (o d)"),
                        tile_of(res, tile), ALU.mult, ALU.add)
                    if k < TOP - 1:
                        me.did(ins)
                        me.wait()
                    else:
                        ins.then_inc(combined, 1)

            def experts(r):
                h = r % HALVES
                regs = [dve.alloc_register(f"dve_owner{r}_{q}") for q in range(2 * SG)]
                dve.wait_ge(owner_ready, r + 1)
                if r == 0:
                    dve.wait_ge(keys_loaded, 16)

                def stage(n, s, g):
                    if s % 2 == 0:
                        dve.load(regs, owner[0:1, h, bass.ds(g * SG, 2 * SG)])
                    if not isinstance(n, int) or n >= UN:
                        dve.wait_ge(h_mm, n - (UN - 1))
                    for q in range(SG):
                        e = dve.snap(regs[s % 2 * SG + q], min_val=0, max_val=E - 1)
                        last = nc.vector.tensor_copy(wk[:, s, q, :], keys_sb[:, bass.ds(e, 1), :].rearrange("p o d -> p (o d)"))
                    last.then_inc(keys_staged, 1)

                def step(g, n, u):
                    if g is None or g + 2 < NG:
                        stage(n + 2, (u + 2) % UN, n - r * NG + 2)
                    if h == 1 and u % 2 == 1 and (g is None or g >= 0):
                        tile_after(g, n, u)

                def tile_after(g, n, u):
                    if g is None:
                        t = loop_turn[0] * (UN // 2) + (u // 2 - LAG)
                        combine(t + (r - 1) * HT, t, (u // 2 - LAG) % 2, t % YR)
                    elif g // 2 >= LAG:
                        t = g // 2 - LAG
                        combine((r - 1) * HT + t, t, t % 2)

                loop_turn = [None]
                first_turn = 1 if r == 0 or h == 1 else 0
                for g in range(-2, first_turn * UN):
                    step(g, r * NG + g, g)
                turns = NG // UN - 1 - first_turn
                per_turn = (UN // 2) * (TOP - 1) if h == 1 else 0
                n_before = me.count
                with dve.Fori(first_turn, first_turn + turns) as i:
                    loop_turn[0] = i
                    me.loop_part = i * per_turn - first_turn * per_turn if per_turn else None
                    for u in range(UN):
                        step(None, i * UN + (r * NG + u), u)
                me.loop_part = None
                assert me.count - n_before == per_turn
                me.count += per_turn * (turns - 1)
                for g in range(NG - UN, NG):
                    step(g, r * NG + g, g)
                if h == 1:
                    for t in range(HT - LAG, HT):
                        combine((r - 1) * HT + t, t, t % 2)

            def attend(pair, between):
                dve.wait_ge(combined, (pair + 1) * HT)
                place_v = (bank67[:, 0, :], bank23[:, 1, :])

                def values_out(c):
                    n = 2 * BC * pair + c
                    dve.wait_ge(chunk_mm, ATT_BASE[pair] + c + 1)
                    nc.vector.tensor_tensor(V[:, c // BC, (c % BC) * CH:(c % BC + 1) * CH, :],
                                            place_v[c % 2].rearrange("p (q d) -> p q d", d=D),
                                            bv_r[:, :].unsqueeze(1).to_broadcast([P, CH, D]), ALU.add).then_inc(v_ready, 1)

                for c in range(2 * BC + 2):
                    if c < 2 * BC:
                        spread(ATT_BASE[pair] + c, c % 2, pair * HT + c * CH)
                    if 0 <= c - 1 < 2 * BC:
                        shifts(ATT_BASE[pair] + c - 1, (c - 1) % 2)
                between(-2)
                for c in range(2 * BC):
                    values_out(c)
                between(-1)

                def largest(j):
                    dve.wait_ge(s_mm, pair * 2 * BT + j + 1)
                    src = (bank45, bank67)[j % 2][:, :, :].rearrange("p a n -> p (a n)")
                    nc.vector.tensor_reduce(nmax[:, j % 2, :], src[:, 0:(j % BT + 1) * P], AX.X, ALU.max,
                                            negate=True).then_inc(max_ready, 1)

                largest(0)
                largest(1)
                for j in range(2 * BT):
                    z = pair * 2 * BT + j
                    if j + 2 < 2 * BT:
                        largest(j + 2)
                    if j < 2:
                        dve.wait_ge(exp_ready, z + 1)
                    me.did(nc.vector.reciprocal(rinv[:, j % 2, :], rowsum[:, j % 4, :]))
                    me.wait()
                    dve.wait_ge(z_mm, z + 1)
                    nc.vector.scalar_tensor_tensor(res[:, z, :], bank23[:, j % 2, 0:D], rinv[:, j % 2, :], res[:, z, :],
                                                   ALU.mult, ALU.add).then_inc(z_added, 1)
                    between(j)
                dve.wait_ge(z_added, 2 * BT * (pair + 1))

            done = [0]

            def combine_next(upto_n):
                while done[0] < min(upto_n, HT):
                    m = HT + done[0]
                    combine(m, m, m % 2)
                    done[0] += 1

            route(0)
            route(1)
            experts(0)
            experts(1)
            attend(0, lambda j: combine_next((j + 3) * 11 // 18))
            route(2, lambda: combine_next(done[0] + 1))
            combine_next(HT)
            attend(1, lambda j: None)
            route(3)
            experts(2)
            experts(3)
            for t in range(HT):
                combine(3 * HT + t, HT + t, t % 2)


_INS = ['L0_attn_x', 'L0_attn_Wq', 'L0_attn_bq', 'L0_attn_Wk', 'L0_attn_bk', 'L0_attn_Wv', 'L0_attn_bv',
        'L0_ffn_expert_sel', 'L0_ffn_keys', 'L0_ffn_values']


def kernel(**inputs):
    import numpy as _np
    import concourse.bacc as _bacc
    from concourse import mybir as _mybir
    from concourse.bass_utils import run_bass_kernel_spmd as _run

    nc = _bacc.Bacc("TRN2", target_bir_lowering=False, num_devices=1)
    arrays, args = {}, []
    for name in _INS:
        a = _np.ascontiguousarray(inputs[name])
        arrays[f"in_{name}_dram"] = a
        args.append(nc.dram_tensor(f"in_{name}_dram", a.shape, _mybir.dt.from_np(a.dtype), kind="ExternalInput").ap())
    shape = inputs['L0_attn_x'].shape
    out = nc.dram_tensor("out_0_dram", shape, _mybir.dt.float32, kind="ExternalOutput").ap()
    moe_attention_macaron_kernel(nc, *args, out)
    r = _run(nc, [arrays], core_ids=[0])
    return r.results[0]["out_0_dram"]
```

```python
import concourse.bass as bass
from concourse import mybir
from contextlib import ExitStack
import math


class SelfSync:

    def __init__(self, eng, sem):
        self.eng, self.sem, self.count, self.loop_part = eng, sem, 0, None

    def did(self, instruction):
        instruction.then_inc(self.sem, 1)
        self.count += 1

    def wait(self):
        self.eng.wait_ge(self.sem, self.count if self.loop_part is None else self.loop_part + self.count)


def moe_attention_macaron_kernel(nc, x, Wq, bq, Wk, bk, Wv, bv, expert_sel, keys, values, out):
    fp32, bf16 = mybir.dt.float32, mybir.dt.bfloat16
    i32, u32 = mybir.dt.int32, mybir.dt.uint32
    ALU, ACT, AX = mybir.AluOpType, mybir.ActivationFunctionType, mybir.AxisListType

    P = 128
    B, S, D = x.shape
    E = keys.shape[0]
    TOP = 4
    NT = B * S // P
    HALVES = 2
    HT = NT // HALVES
    ROUTES = 2 * HALVES
    CH = 4
    RC = HT // CH
    BT = S // P
    BC = BT // CH
    SG = 4
    NG = -(-(HT * TOP + E - 1) // SG)
    SLOTS = NG * SG * P
    UN = 4
    YR = 8
    LAG = UN // 2
    EPS = 1e-5
    SCALE = 1.0 / math.sqrt(D)
    NEVER = -3.0e38
    NONE = -200.0
    LOGIT_CAP = 17.5

    ROUTE_BASE = [0, RC, 2 * RC + 2 * BC, 3 * RC + 4 * BC]
    ATT_BASE = [2 * RC, 3 * RC + 2 * BC]

    x_t = x.rearrange("b (t p) d -> p (b t) d", p=P)
    out_t = out.rearrange("b (t p) d -> p (b t) d", p=P)

    ctx = ExitStack()
    with ctx:
        def sb(name, shape, dt=fp32):
            return ctx.enter_context(nc.sbuf_tensor(name, shape, dt))

        def pb(name, shape, dt=fp32):
            return ctx.enter_context(nc.psum_tensor(name, shape, dt))

        def sem(name):
            return ctx.enter_context(nc.semaphore(name))

        Xs = [nc.dram_tensor(f"sorted_in_{h}", [SLOTS, D], fp32).ap() for h in range(HALVES)]
        Ys = [nc.dram_tensor(f"sorted_out_{h}", [SLOTS, D], fp32).ap() for h in range(HALVES)]
        Xs_g = [a.rearrange("(p g q) d -> g p q d", q=SG, p=P) for a in Xs]
        Ys_g = [a.rearrange("(p g q) d -> g p q d", q=SG, p=P) for a in Ys]

        res = sb("res", [P, NT, D])
        xln = sb("xln", [P, NT, D])
        keys_sb = sb("keys_sb", [P, E, P])
        vals_sb = sb("vals_sb", [P, E, D])
        xin = sb("xin", [P, UN, SG, D])
        wk = sb("wk", [P, UN, SG, P])
        sxT = sb("sxT", [P, 2, SG * P])
        hT = sb("hT", [P, 2, SG * P])
        yout = sb("yout", [P, 2, SG, D])
        yg = sb("yg", [P, YR, TOP, D])
        ident = sb("ident", [P, P])
        ident_b = sb("ident_b", [P, P], bf16)
        later = sb("later", [P, P], bf16)
        before = sb("before", [P, P], bf16)
        ones_b = sb("ones_b", [P, P], bf16)
        tile_rows = sb("tile_rows", [E, P], bf16)
        upto = sb("upto", [E, E], bf16)
        iota_ki = sb("iota_ki", [P, TOP], i32)
        iota_k = sb("iota_k", [P, TOP])
        iota_ji = sb("iota_ji", [E, NG * SG], i32)
        iota_j = sb("iota_j", [E, NG * SG])
        restart = sb("restart", [P, E, HT], bf16)
        eps_c = sb("eps_c", [P, 1])
        wT = sb("wT", [P, 4, P])
        bq_c = sb("bq_c", [P, 1])
        bq_s = sb("bq_s", [P, 1])
        bk_c = sb("bk_c", [P, 1])
        bv_r = sb("bv_r", [P, D])
        stats = sb("stats", [P, 2, CH, 6])
        msum, mdif, dev2, mean, mdif2, var = (sb(n, [P, 2, CH]) for n in ("msum", "mdif", "dev2", "mean", "mdif2", "var"))
        lnv = sb("lnv", [P, 2, CH])
        shift = sb("shift", [P, 2, CH])
        rstd = sb("rstd", [P, 2, CH])
        nT = sb("nT", [P, 2, CH * P])
        QT = sb("QT", [P, 2, S])
        KT = sb("KT", [P, 2, S])
        V = xin[:, :, :, :].rearrange("p u q d -> p (u q) d").rearrange("p (a b) d -> p a b d", a=2)
        Pm = sb("Pm", [P, 2, S])
        w_in = Pm[:, 0, 0:4 * D].rearrange("p (j d) -> p j d", j=4)
        PT = sb("PT", [P, 2, S])
        nmax = sb("nmax", [P, 2, 1])
        rowsum = sb("rowsum", [P, 4, 1])
        rinv = sb("rinv", [P, 2, 1])
        lg = sb("lg", [P, NT, E + TOP])
        left = sb("left", [P, CH, E + TOP])
        top = sb("top", [P, NT, 2, TOP])
        chosen = sb("chosen", [P, CH, 2, TOP])
        topi = sb("topi", [P, HT, 8], u32)
        prod = sb("prod", [P, E, HT])
        mask = sb("mask", [P, E, HT], bf16)
        runs = sb("runs", [P, E, HT], bf16)
        slot = sb("slot", [P, HT, 8])
        slot_i, slot_tile = (sb(n, [P, HT, TOP], i32) for n in ("slot_i", "slot_tile"))
        pos = sb("pos", [P, NT, TOP], u32)
        ge = sb("ge", [P, NT, TOP])
        gk = sb("gk", [P, HT, TOP])
        rank = sb("rank", [P, HT, TOP])
        slot_row = rank
        above, placed, gsel = (prod[:, i * E // 4:(i + 1) * E // 4, :].rearrange("p (t u) (a b) -> p t (u a b)", t=HT, a=TOP)
                               .rearrange("p t (a b) -> p t a b", a=TOP) for i in range(3))
        gate = sb("gate", [P, NT, TOP])
        cnt_i = sb("cnt_i", [E, 1], i32)
        cnt_s = sb("cnt_s", [E, 1], i32)
        tiles_b = sb("tiles_b", [E, 1], bf16)
        end_c = sb("end_c", [E, 1])
        start_c = sb("start_c", [E, 1])
        start_d = sb("start_d", [E, E], bf16)
        past = sb("past", [E, NG * SG], bf16)
        owner = sb("owner", [1, HALVES, NG * SG], i32)
        zero = PT[:, :, :].rearrange("p a n -> p (a n)")

        bank01 = pb("bank01", [P, 2, 512])
        bank23 = pb("bank23", [P, 2, 512])
        bank45 = pb("bank45", [P, 2, 512])
        bank67 = pb("bank67", [P, 2, 512])

        def turned_place(r, c):
            if r < HALVES:
                return bank01[:, c % 2, :]
            return bank45[:, 0, :] if c == 2 else bank01[:, 1, :]

        def logits_place(r, c):
            if r < HALVES:
                return bank23[:, c % 2, :]
            return (bank45, bank67)[c % 2][:, 1, :]

        x_in = [sem(f"x_in{c}") for c in range(NT // CH)]
        w_loaded = sem("w_loaded")
        keys_loaded = sem("keys_loaded")
        vals_loaded = sem("vals_loaded")
        filled = [sem(f"filled{h}") for h in range(HALVES)]
        zero_ready = sem("zero_ready")
        const_ready = sem("const_ready")
        pool_self = sem("pool_self")
        sel_loaded = sem("sel_loaded")
        sel_turned = sem("sel_turned")
        sel_ready = sem("sel_ready")
        w_turned = sem("w_turned")
        w_ready = sem("w_ready")
        stats_ready = sem("stats_ready")
        ln_ready = sem("ln_ready")
        rstd_ready = sem("rstd_ready")
        shift_ready = sem("shift_ready")
        normed = sem("normed")
        normed_too = sem("normed_too")
        turned = sem("turned")
        nT_ready = sem("nT_ready")
        chunk_mm = sem("chunk_mm")
        logits_out = sem("logits_out")
        top_ready = sem("top_ready")
        gate_exp = sem("gate_exp")
        gates_ready = sem("gates_ready")
        runs_ready = sem("runs_ready")
        cnt_mm = sem("cnt_mm")
        tiles_ready = sem("tiles_ready")
        end_mm = sem("end_mm")
        start_ready = sem("start_ready")
        owner_mm = sem("owner_mm")
        owner_ready = sem("owner_ready")
        rank_mm = sem("rank_mm")
        ranks_out = sem("ranks_out")
        pos_ready = sem("pos_ready")
        scattered = [sem(f"scattered{h}") for h in range(HALVES)]
        xin_loaded = [sem(f"xin_loaded{s}") for s in range(UN)]
        slots_turned = sem("slots_turned")
        sxT_ready = sem("sxT_ready")
        keys_staged = sem("keys_staged")
        h_mm = sem("h_mm")
        h_ready = sem("h_ready")
        y_mm = sem("y_mm")
        y_ready = sem("y_ready")
        y_stored = [sem(f"y_stored{s}") for s in range(2)]
        gathered = [sem(f"gathered{s}") for s in range(2)]
        combined = sem("combined")
        q_mm, k_mm = sem("q_mm"), sem("k_mm")
        q_ready, k_ready, v_ready = sem("q_ready"), sem("k_ready"), sem("v_ready")
        s_mm = sem("s_mm")
        max_ready = sem("max_ready")
        exp_ready = sem("exp_ready")
        p_turned = sem("p_turned")
        pT_ready = sem("pT_ready")
        z_mm = sem("z_mm")
        z_added = sem("z_added")
        dve_self = sem("dve_self")
        out_stored = sem("out_stored")

        block = ctx.enter_context(nc.Block())

        def tile_of(buf, t):
            return buf[:, bass.ds(t, 1), :].rearrange("p o d -> p (o d)")

        def skewed(eng, r, step, begin, rest):
            if begin:
                for g in range(-2, 0):
                    step(g, r * NG + g, g)
            if not rest:
                return
            if r == 0:
                for g in range(UN):
                    step(g, g, g)
            first_turn = 1 if r == 0 else 0
            with eng.Fori(first_turn, NG // UN - 1) as i:
                for u in range(UN):
                    step(None, i * UN + (r * NG + u), u)
            for g in range(NG - UN, NG):
                step(g, r * NG + g, g)

        @block.sync
        def _(sp):
            def load_x(c):
                sp.dma_start(res[:, c * CH:(c + 1) * CH, :], x_t[:, c * CH:(c + 1) * CH, :]).then_inc(x_in[c], 16)

            def load_weights():
                for j, w in enumerate((Wq, Wk, Wv)):
                    sp.dma_start(w_in[:, j, :], w).then_inc(w_loaded, 16)
                sp.dma_start(bq_c[:, :], bq.rearrange("(p o) -> p o", o=1)).then_inc(w_loaded, 16)
                sp.dma_start(bk_c[:, :], bk.rearrange("(p o) -> p o", o=1)).then_inc(w_loaded, 16)
                sp.dma_start(bv_r[:, :], bv.rearrange("(o d) -> o d", o=1).to_broadcast([P, D])).then_inc(w_loaded, 16)

            for c in range(RC):
                load_x(c)
            sp.wait_ge(zero_ready, 1)
            rows = P * zero.shape[1] // D
            for h in range(HALVES):
                for k in range(SLOTS // rows):
                    sp.dma_start(Xs[h][k * rows:(k + 1) * rows, :].rearrange("(p a) d -> p (a d)", p=P),
                                 zero[:, :]).then_inc(filled[h], 16)
                    if h == 0 and k == 1:
                        load_weights()
                if h == 0:
                    for c in range(RC, NT // CH):
                        load_x(c)
                    sp.dma_start(keys_sb[:, :, :], keys.rearrange("k d e -> d k e")).then_inc(keys_loaded, 16)
                    sp.dma_start(vals_sb[:, :, :], values.rearrange("k e v -> e k v")).then_inc(vals_loaded, 16)

            def scatter_done(r):
                sp.wait_ge(scattered[r % HALVES], 16 * TOP * HT * (r // HALVES + 1))

            for r in range(ROUTES):
                h = r % HALVES
                n0 = r * NG

                def load(g, n, s, h=h):
                    if not isinstance(n, int) or n >= UN:
                        sp.wait_ge(slots_turned, n - (UN - 1))
                    sp.dma_start(xin[:, s, :, :], Xs_g[h][bass.ds(g, 1)].rearrange("o p q d -> (o p) q d")
                                 if not isinstance(g, int) else Xs_g[h][g]).then_inc(xin_loaded[s], 16)

                def store(g, n, s):
                    sp.wait_ge(y_ready, n + 1)
                    sp.dma_start(Ys_g[h][bass.ds(g, 1)].rearrange("o p q d -> (o p) q d")
                                 if not isinstance(g, int) else Ys_g[h][g],
                                 yout[:, s, :, :]).then_inc(y_stored[s], 16)

                if h == 0:
                    scatter_done(r)
                    if r >= HALVES:
                        sp.wait_ge(z_added, 2 * BT * (NT // HT))
                    for g in range(UN):
                        load(g, n0 + g, g % UN)
                if r >= HALVES:
                    sp.wait_ge(combined, HT * (r - HALVES + 1))
                for g in range(UN, UN + 2):
                    load(g, n0 + g, g % UN)
                turns = (NG - UN - 2) // UN
                with sp.Fori(0, turns) as i:
                    for u in range(UN):
                        load(i * UN + (UN + 2 + u), i * UN + (n0 + UN + 2 + u), (2 + u) % UN)
                        store(i * UN + u, i * UN + (n0 + u), u % 2)
                for g in range(turns * UN, NG):
                    if g + UN + 2 < NG:
                        load(g + UN + 2, n0 + g + UN + 2, (g + UN + 2) % UN)
                    store(g, n0 + g, g % 2)
                    if h == 0 and g == NG - 3:
                        scatter_done(r + 1)
                        for k in range(UN):
                            load(k, n0 + NG + k, k, h=1)

            for c in range(NT // CH):
                sp.wait_ge(combined, NT + (c + 1) * CH)
                sp.dma_start(out_t[:, c * CH:(c + 1) * CH, :], res[:, c * CH:(c + 1) * CH, :]).then_inc(out_stored, 16)
            sp.wait_ge(out_stored, 16 * (NT // CH))

        @block.gpsimd
        def _(gp):
            me = SelfSync(gp, pool_self)
            me.did(nc.gpsimd.memset(ident[:, :], 0.0))
            me.did(nc.gpsimd.memset(ident_b[:, :], 0.0))
            me.did(nc.gpsimd.memset(later[:, :], 0.0))
            me.did(nc.gpsimd.memset(before[:, :], 0.0))
            me.did(nc.gpsimd.memset(upto[:, :], 1.0))
            me.did(nc.gpsimd.memset(restart[:, :, :], 1.0))
            me.wait()
            for buf, op, fill, step, mult, n in (
                    (ident, ALU.not_equal, 1.0, -1, 1, P), (ident_b, ALU.not_equal, 1.0, -1, 1, P),
                    (later, ALU.is_ge, NEVER, -1, 1, P), (before, ALU.is_gt, -1.0, 1, -1, P),
                    (upto, ALU.is_ge, 0.0, 1, -1, E)):
                nc.gpsimd.affine_select(out=buf[:, :], in_=buf[:, :], compare_op=op, fill=fill, base=0,
                                        pattern=[[step, n]], channel_multiplier=mult).then_inc(const_ready, 1)
            nc.gpsimd.memset(restart[:, :, 0:1], 0.0).then_inc(const_ready, 1)
            nc.gpsimd.memset(ones_b[:, :], 1.0).then_inc(const_ready, 1)
            nc.gpsimd.memset(tile_rows[:, :], float(P)).then_inc(const_ready, 1)
            nc.gpsimd.memset(eps_c[:, :], EPS).then_inc(const_ready, 1)
            nc.gpsimd.iota(iota_ki[:, :], pattern=[[1, TOP]], base=0, channel_multiplier=0).then_inc(const_ready, 1)
            nc.gpsimd.iota(iota_ji[:, :], pattern=[[1, NG * SG]], base=0, channel_multiplier=0).then_inc(const_ready, 1)

            def scatter(r):
                h = r % HALVES
                if r < HALVES:
                    gp.wait_ge(filled[h], 16 * (SLOTS * D // (P * zero.shape[1])))
                else:
                    gp.wait_ge(slots_turned, NG * (r - HALVES + 1))
                for t in range(h * HT, (h + 1) * HT):
                    if t % HT in (0, CH):
                        gp.wait_ge(pos_ready, 2 * r + 1 + t % HT // CH)
                    for k in range(TOP):
                        nc.gpsimd.indirect_dma_start(
                            out=Xs[h], out_offset=bass.IndirectOffsetOnAxis(ap=pos[:, t, k:k + 1], axis=0),
                            in_=xln[:, t, :], in_offset=None).then_inc(scattered[h], 16)

            def gather(r):
                h = r % HALVES
                for s in range(2):
                    gp.wait_ge(y_stored[s], 16 * (NG // 2) * (r + 1))
                for t in range(HT):
                    m = r * HT + t
                    if m >= 2:
                        gp.wait_ge(gathered[m % 2], 16 * TOP * (m // 2))
                    if m >= YR:
                        gp.wait_ge(combined, m - YR + 1)
                    for k in range(TOP):
                        nc.gpsimd.indirect_dma_start(
                            out=yg[:, m % YR, k, :], out_offset=None, in_=Ys[h],
                            in_offset=bass.IndirectOffsetOnAxis(ap=pos[:, h * HT + t, k:k + 1], axis=0),
                        ).then_inc(gathered[m % 2], 16)

            for f in range(2):
                scatter(2 * f)
                scatter(2 * f + 1)
                gather(2 * f)
                gather(2 * f + 1)

        @block.tensor
        def _(pe):
            def turn_sel():
                pe.wait_ge(sel_loaded, 16)
                nc.tensor.transpose(bank67[:, 0, 0:E], w_in[0:E, 3, :], ident[0:E, 0:E]).then_inc(sel_turned, 1)

            def turn_weights():
                pe.wait_ge(w_loaded, 16 * 6)
                pe.wait_ge(owner_ready, 1)
                for j in range(3):
                    last = nc.tensor.transpose(bank67[:, 0, j * P:(j + 1) * P], w_in[:, j, :], ident[:, :])
                last.then_inc(w_turned, 1)

            def turn_chunk(idx, to, tile0):
                pe.wait_ge(normed, idx + 1)
                for r in range(HALVES, ROUTES):
                    if idx == ROUTE_BASE[r] + RC - 1:
                        pe.wait_ge(normed_too, r - HALVES + 1)
                if idx >= 2:
                    pe.wait_ge(nT_ready, idx - 1)
                for q in range(CH):
                    last = nc.tensor.transpose(to[:, q * P:(q + 1) * P], xln[:, tile0 + q, :], ident[:, :])
                last.then_inc(turned, 1)

            def route_turn(r, c):
                turn_chunk(ROUTE_BASE[r] + c, turned_place(r, c), (r % HALVES) * HT + c * CH)

            def route_logits(r, c):
                pe.wait_ge(nT_ready, ROUTE_BASE[r] + c + 1)
                if r * RC + c >= 2:
                    pe.wait_ge(logits_out, r * RC + c - 1)
                to = logits_place(r, c)
                for q in range(CH):
                    last = nc.tensor.matmul(to[:, q * E:(q + 1) * E], nT[:, c % 2, q * P:(q + 1) * P],
                                            wT[:, 3, 0:E], start=True, stop=True)
                last.then_inc(chunk_mm, 1)

            def route(r):
                if r >= HALVES:
                    route_turn(r, RC - 1)
                    route_logits(r, RC - 1)
                    if r == HALVES + 1:
                        experts(HALVES, rest=False)
                else:
                    if r == 0:
                        pe.wait_ge(const_ready, 11)
                    for c in range(RC + 1):
                        if c < RC:
                            route_turn(r, c)
                        if r == 0 and c == 0:
                            turn_sel()
                            pe.wait_ge(sel_ready, 1)
                        if c >= 1:
                            route_logits(r, c - 1)
                if r == 1:
                    pe.wait_ge(w_ready, 1)
                pe.wait_ge(runs_ready, r + 1)
                nc.tensor.matmul(bank67[0:E, 0, 0:1], runs[:, :, HT - 1], ones_b[:, 0:1],
                                 start=True, stop=True).then_inc(cnt_mm, 1)
                eh = E // 2
                for j in range(2):
                    nc.tensor.matmul(bank45[:, j, :], before[:, :], mask[:, j * eh:(j + 1) * eh, :].rearrange("p e t -> p (e t)"),
                                     start=True, stop=False)
                    nc.tensor.matmul(bank45[:, j, :], ones_b[:, :], runs[:, j * eh:(j + 1) * eh, :].rearrange("p e t -> p (e t)"),
                                     start=False, stop=False)
                pe.wait_ge(tiles_ready, r + 1)
                nc.tensor.matmul(bank67[0:E, 0, 0:1], upto[:, :], tiles_b[:, :], start=True, stop=True).then_inc(end_mm, 1)
                pe.wait_ge(start_ready, r + 1)
                nc.tensor.matmul(bank67[0:1, 1, 0:NG * SG], ones_b[0:E, 0:1], past[:, :],
                                 start=True, stop=True).then_inc(owner_mm, 1)
                for j in range(2):
                    last = nc.tensor.matmul(bank45[:, j, :].rearrange("p (e t) -> p e t", t=HT), tile_rows[:, :],
                                            start_d[:, j * eh:(j + 1) * eh].unsqueeze(2).to_broadcast([E, eh, HT]),
                                            start=False, stop=True)
                last.then_inc(rank_mm, 1)

            owner_regs = [pe.alloc_register(f"pe_owner{q}") for q in range(SG)]

            def experts(r, begin=True, rest=True):
                h = r % HALVES
                regs = owner_regs
                pe.wait_ge(owner_ready, r + 1)
                if r == 0:
                    pe.wait_ge(vals_loaded, 16)

                def turn(n, s, u):
                    pe.wait_ge(xin_loaded[u], u_count(n, u))
                    if not isinstance(n, int) or n >= 2:
                        pe.wait_ge(sxT_ready, n - 1)
                    for q in range(SG):
                        last = nc.tensor.transpose(bank01[:, s, q * P:(q + 1) * P], xin[:, u, q, :], ident[:, :])
                    last.then_inc(slots_turned, 1)

                def u_count(n, u):
                    return (n - u) * (16 // UN) + 16 if not isinstance(n, int) else 16 * (n // UN + 1)

                def first(n, s, u):
                    pe.wait_ge(sxT_ready, n + 1)
                    pe.wait_ge(keys_staged, n + 1)
                    if not isinstance(n, int) or n >= 2:
                        pe.wait_ge(h_ready, n - 1)
                    for q in range(SG):
                        last = nc.tensor.matmul(bank23[:, s, q * P:(q + 1) * P], wk[:, u, q, :],
                                                sxT[:, s, q * P:(q + 1) * P], start=True, stop=True)
                    last.then_inc(h_mm, 1)

                def second(n, s, g):
                    pe.load(regs, owner[0:1, h, bass.ds(g * SG, SG)])
                    pe.wait_ge(h_ready, n + 1)
                    if not isinstance(n, int) or n >= 2:
                        pe.wait_ge(y_ready, n - 1)
                    for q in range(SG):
                        e = pe.snap(regs[q], min_val=0, max_val=E - 1)
                        last = nc.tensor.matmul(bank45[:, s, q * D:(q + 1) * D], hT[:, s, q * P:(q + 1) * P],
                                                vals_sb[:, bass.ds(e, 1), :].rearrange("p o d -> p (o d)"),
                                                start=True, stop=True)
                    last.then_inc(y_mm, 1)

                def step(g, n, u):
                    if g is None or g + 2 < NG:
                        turn(n + 2, u % 2, (u + 2) % UN)
                    if g is None or (g >= -1 and g + 1 < NG):
                        first(n + 1, (u + 1) % 2, (u + 1) % UN)
                    if g is None or g >= 0:
                        second(n, u % 2, n - r * NG)

                if rest and h == 0:
                    pe.wait_ge(ranks_out, r + HALVES)
                skewed(pe, r, step, begin, rest)

            def attend(pair):
                base = ATT_BASE[pair]
                place = ((bank67[:, 1, :], bank23[:, 0, :], bank23[:, 1, :]),
                         (bank45[:, 0, :], bank45[:, 1, :], bank67[:, 0, :]))

                def project(c):
                    n = 2 * BC * pair + c
                    pe.wait_ge(nT_ready, base + c + 1)
                    if c == 0:
                        pe.wait_ge(owner_ready, HALVES + pair)
                    if c == 1:
                        pe.wait_ge(ranks_out, HALVES + pair)
                    if c >= 2:
                        pe.wait_ge(q_ready, n - 1)
                        pe.wait_ge(k_ready, n - 1)
                        pe.wait_ge(v_ready, n - 1)
                    to_q, to_k, to_v = place[c % 2]
                    nc.tensor.matmul(to_q, wT[:, 0, :], nT[:, c % 2, :], start=True, stop=True).then_inc(q_mm, 1)
                    nc.tensor.matmul(to_k, wT[:, 1, :], nT[:, c % 2, :], start=True, stop=True).then_inc(k_mm, 1)
                    for q in range(CH):
                        last = nc.tensor.matmul(to_v[:, q * D:(q + 1) * D], nT[:, c % 2, q * P:(q + 1) * P],
                                                wT[:, 2, :], start=True, stop=True)
                    last.then_inc(chunk_mm, 1)

                for c in range(2 * BC + 1):
                    if c < 2 * BC:
                        turn_chunk(base + c, bank01[:, c % 2, :], pair * HT + c * CH)
                    if c >= 1:
                        project(c - 1)

                score_bank = (bank45, bank67)

                def scores(j):
                    z, row, i = pair * 2 * BT + j, j // BT, j % BT
                    if j == 0:
                        pe.wait_ge(q_ready, 2 * BC * (pair + 1))
                        pe.wait_ge(k_ready, 2 * BC * (pair + 1))
                        pe.wait_ge(v_ready, 2 * BC * (pair + 1))
                    if j >= 2:
                        pe.wait_ge(exp_ready, z - 1)
                    w = (i + 1) * P
                    for c in range(-(-w // 512)):
                        n = min(512, w - c * 512)
                        diag = c * 512 + n == w
                        last = nc.tensor.matmul(score_bank[j % 2][:, c, 0:n], QT[:, row, i * P:(i + 1) * P],
                                                KT[:, row, c * 512:c * 512 + n], start=True, stop=not diag)
                        if diag:
                            last = nc.tensor.matmul(score_bank[j % 2][:, c, n - P:n], ident_b[:, :], later[:, :],
                                                    start=False, stop=True)
                    last.then_inc(s_mm, 1)

                def turn_probs(j):
                    z, i = pair * 2 * BT + j, j % BT
                    pe.wait_ge(exp_ready, z + 1)
                    if z >= 1:
                        pe.wait_ge(pT_ready, z)
                    for n in range(i + 1):
                        last = nc.tensor.transpose(bank01[:, n // 4, (n % 4) * P:(n % 4 + 1) * P],
                                                   Pm[:, j % 2, n * P:(n + 1) * P], ident[:, :])
                    last.then_inc(p_turned, 1)

                def weigh(j):
                    z, row, i = pair * 2 * BT + j, j // BT, j % BT
                    pe.wait_ge(pT_ready, z + 1)
                    if z >= 2:
                        pe.wait_ge(z_added, z - 1)
                    for n in range(i + 1):
                        last = nc.tensor.matmul(bank23[:, j % 2, 0:D], PT[:, j % 2, n * P:(n + 1) * P], V[:, row, n, :],
                                                start=(n == 0), stop=(n == i))
                    last.then_inc(z_mm, 1)

                r = HALVES + pair
                scores(0)
                scores(1)
                turn_probs(0)
                for j in range(2 * BT):
                    if j in (BT + 2, BT + 3):
                        pe.wait_ge(logits_out, r * RC + j - BT - 1)
                    if j + 2 < 2 * BT:
                        scores(j + 2)
                    if j == BT + 3:
                        pe.wait_ge(nT_ready, ROUTE_BASE[r] + 2)
                    if j + 1 < 2 * BT:
                        turn_probs(j + 1)
                    if j == BT + 2:
                        route_logits(r, 1)
                    weigh(j)
                    if j == BT:
                        route_turn(r, 0)
                    if j == BT + 1:
                        route_logits(r, 0)
                        route_turn(r, 1)
                route_turn(r, 2)
                route_logits(r, 2)

            route(0)
            turn_weights()
            route(1)
            experts(0)
            experts(1)
            attend(0)
            route(2)
            attend(1)
            route(3)
            experts(2, begin=False)
            experts(3)

        @block.scalar
        def _(act):
            nc.scalar.preload_act_table_set("natural_log_exp_and_others")
            act.dma_start(w_in[0:E, 3, :], expert_sel).then_inc(sel_loaded, 16)
            act.wait_ge(const_ready, 11)

            def sel_out():
                act.wait_ge(sel_turned, 1)
                nc.scalar.copy(wT[:, 3, 0:E], bank67[:, 0, 0:E]).then_inc(sel_ready, 1)

            def weights_out():
                act.wait_ge(w_loaded, 16 * 6)
                nc.scalar.mul(bq_s[:, :], bq_c[:, :], SCALE)
                act.wait_ge(w_turned, 1)
                nc.scalar.copy(wT[:, 0:3, :], bank67[:, 0, 0:3 * P].rearrange("p (j n) -> p j n", j=3)).then_inc(w_ready, 1)

            def inverse_spread(idx, c):
                act.wait_ge(stats_ready, idx + 1)
                nc.scalar.activation(lnv[:, c, :], var[:, c, :], ACT.Ln, bias=eps_c[:, 0:1]).then_inc(ln_ready, 1)
                act.wait_ge(ln_ready, idx + 1)
                nc.scalar.activation(rstd[:, c, :], lnv[:, c, :], ACT.Exp, scale=-0.5).then_inc(rstd_ready, 1)

            def normalise(idx, c, tile0, rows=CH):
                act.wait_ge(shift_ready, idx + 1)
                for q in range(rows):
                    last = nc.scalar.activation(xln[:, tile0 + q, :], res[:, tile0 + q, :], ACT.Identity,
                                                bias=shift[:, c, q:q + 1], scale=rstd[:, c, q:q + 1])
                last.then_inc(normed, 1)

            def copy_turned(idx, c, place):
                act.wait_ge(turned, idx + 1)
                if idx >= 2:
                    act.wait_ge(chunk_mm, idx - 1)
                nc.scalar.copy(nT[:, c, :], place).then_inc(nT_ready, 1)

            def norm_steps(base, chunks, tile0, after=None, once=None, ahead=False):
                def turned_out(c):
                    copy_turned(base + c, c % 2, bank01[:, c % 2, :])
                    if after is not None:
                        after(c)

                for c in range(chunks + 2):
                    if c < chunks and (c > 0 or not ahead):
                        inverse_spread(base + c, c % 2)
                    if 0 <= c - 1 < chunks and (c > 1 or not ahead):
                        normalise(base + c - 1, (c - 1) % 2, tile0 + (c - 1) * CH)
                    if c == 1 and once is not None:
                        once()
                    if c >= 2:
                        turned_out(c - 2)

            def route_part(r, c, part):
                idx = ROUTE_BASE[r] + c
                if part == 0:
                    inverse_spread(idx, c % 2)
                elif part == 1:
                    normalise(idx, c % 2, (r % HALVES) * HT + c * CH, CH // 2 if c == RC - 1 else CH)
                else:
                    copy_turned(idx, c % 2, turned_place(r, c))

            def route(r):
                h = r % HALVES
                if r < HALVES:
                    norm_steps(ROUTE_BASE[r], RC, h * HT, once=sel_out if r == 0 else None)
                else:
                    route_part(r, RC - 2, 2)
                    route_part(r, RC - 1, 0)
                    route_part(r, RC - 1, 1)
                    route_part(r, RC - 1, 2)
                if r == HALVES + 1:
                    experts(HALVES, rest=False)
                act.wait_ge(top_ready, (r + 1) * RC)
                if r >= HALVES:
                    act.wait_ge(gates_ready, r - 1)
                half = slice(h * HT, (h + 1) * HT)
                nc.scalar.activation(ge[:, half, :], top[:, half, 0, :], ACT.Exp, scale=-1.0).then_inc(gate_exp, 1)

            def experts(r, begin=True, rest=True):
                def step(g, n, u):
                    if g is None or g + 2 < NG:
                        m = n + 2
                        act.wait_ge(slots_turned, m + 1)
                        if not isinstance(m, int) or m >= 2:
                            act.wait_ge(h_mm, m - 1)
                        nc.scalar.copy(sxT[:, u % 2, :], bank01[:, u % 2, :]).then_inc(sxT_ready, 1)
                    if g is None or (g >= -1 and g + 1 < NG):
                        m = n + 1
                        act.wait_ge(h_mm, m + 1)
                        if not isinstance(m, int) or m >= 2:
                            act.wait_ge(y_mm, m - 1)
                        nc.scalar.activation(hT[:, (u + 1) % 2, :], bank23[:, (u + 1) % 2, :], ACT.Relu).then_inc(h_ready, 1)
                    if g is None or g >= 0:
                        act.wait_ge(y_mm, n + 1)
                        if not isinstance(n, int):
                            act.wait_ge(y_stored[u % 2], n * 8 - 8 * (u % 2))
                        elif n >= 2:
                            act.wait_ge(y_stored[u % 2], 16 * (n // 2))
                        nc.scalar.copy(yout[:, u % 2, :, :].rearrange("p q d -> p (q d)"), bank45[:, u % 2, :]).then_inc(y_ready, 1)
                    if r == 1 and g == NG - 2:
                        inverse_spread(ATT_BASE[0], 0)
                        act.wait_ge(scattered[0], 16 * TOP * HT)
                        normalise(ATT_BASE[0], 0, 0)

                skewed(act, r, step, begin, rest)

            def attend(pair):
                score_bank = (bank45, bank67)
                place = ((bank67[:, 1, :], bank23[:, 0, :]), (bank45[:, 0, :], bank45[:, 1, :]))

                def project_out(c):
                    n = 2 * BC * pair + c
                    row, half = c // BC, c % BC
                    to_q, to_k = place[c % 2]
                    act.wait_ge(q_mm, n + 1)
                    nc.scalar.activation(QT[:, row, half * 512:(half + 1) * 512], to_q, ACT.Identity,
                                         bias=bq_s[:, 0:1], scale=SCALE).then_inc(q_ready, 1)
                    act.wait_ge(k_mm, n + 1)
                    nc.scalar.activation(KT[:, row, half * 512:(half + 1) * 512], to_k, ACT.Identity,
                                         bias=bk_c[:, 0:1]).then_inc(k_ready, 1)

                base = ATT_BASE[pair]
                if pair == 0:
                    norm_steps(base, 2 * BC, 0, lambda c: project_out(c - 1) if c else None, ahead=True)
                else:
                    act.wait_ge(scattered[1], 16 * TOP * HT)
                    spread_of = lambda c: inverse_spread(base + c, c % 2)
                    rows_of = lambda c: normalise(base + c, c % 2, HT + c * CH)
                    turned_of = lambda c: copy_turned(base + c, c % 2, bank01[:, c % 2, :])
                    for c in range(2 * BC + 2):
                        if c >= 2:
                            turned_of(c - 2)
                        if c >= 3:
                            project_out(c - 3)
                        if 1 <= c <= 2 * BC:
                            rows_of(c - 1)
                        if c < 2 * BC:
                            spread_of(c)
                project_out(2 * BC - 1)

                def exps(j):
                    z, i = pair * 2 * BT + j, j % BT
                    act.wait_ge(max_ready, z + 1)
                    if z >= 2:
                        act.wait_ge(p_turned, z - 1)
                    if z >= 4:
                        act.wait_ge(z_added, z - 3)
                    w = (i + 1) * P
                    nc.scalar.activation(Pm[:, j % 2, 0:w], score_bank[j % 2][:, :, :].rearrange("p a n -> p (a n)")[:, 0:w],
                                         ACT.Exp, bias=nmax[:, j % 2, :], accum_out=rowsum[:, j % 4, :]).then_inc(exp_ready, 1)

                def probs_out(j):
                    z, i = pair * 2 * BT + j, j % BT
                    act.wait_ge(p_turned, z + 1)
                    if z >= 2:
                        act.wait_ge(z_mm, z - 1)
                    if z == 0:
                        act.wait_ge(filled[HALVES - 1], 16 * (SLOTS * D // (P * zero.shape[1])))
                    w = (i + 1) * P
                    nc.scalar.copy(PT[:, j % 2, 0:w], bank01[:, :, :].rearrange("p a n -> p (a n)")[:, 0:w]).then_inc(pT_ready, 1)

                along = {BT - 3: ((0, 0),), BT - 2: ((0, 1),), BT - 1: ((1, 0),), BT: ((0, 2), (1, 1)),
                         BT + 1: ((1, 2),), BT + 4: ((2, 0),), 2 * BT - 2: ((2, 1),)}
                exps(0)
                exps(1)
                probs_out(0)
                for j in range(2 * BT):
                    if j + 1 < 2 * BT:
                        probs_out(j + 1)
                    if j + 2 < 2 * BT:
                        exps(j + 2)
                    for c, part in along.get(j, ()):
                        route_part(HALVES + pair, c, part)

            route(0)
            weights_out()
            route(1)
            experts(0)
            experts(1)
            attend(0)
            route(2)
            attend(1)
            route(3)
            experts(2, begin=False)
            experts(3)

        @block.vector
        def _(dve):
            me = SelfSync(dve, dve_self)
            nc.vector.memset(zero, 0.0).then_inc(zero_ready, 1)

            def spread(idx, c, tile0, first=0):
                spread_rows(c, tile0, range(first, CH))
                me.wait()
                even, odd = stats[:, c, :, 1], stats[:, c, :, 4]
                me.did(nc.vector.tensor_tensor(msum[:, c, :], even, odd, ALU.add))
                me.did(nc.vector.tensor_tensor(mdif[:, c, :], even, odd, ALU.subtract))
                me.did(nc.vector.tensor_tensor(dev2[:, c, :], stats[:, c, :, 2], stats[:, c, :, 5], ALU.add))
                me.wait()
                me.did(nc.vector.tensor_scalar(mean[:, c, :], msum[:, c, :], -0.5, None, ALU.mult))
                me.did(nc.vector.scalar_tensor_tensor(mdif2[:, c, :], mdif[:, c, :], 0.25, mdif[:, c, :], ALU.mult, ALU.mult))
                me.wait()
                nc.vector.scalar_tensor_tensor(var[:, c, :], dev2[:, c, :], 1.0 / D, mdif2[:, c, :],
                                               ALU.mult, ALU.add).then_inc(stats_ready, 1)

            def spread_rows(c, tile0, rows):
                for q in rows:
                    me.did(nc.vector.bn_stats(stats[:, c, q, :], res[:, tile0 + q, :]))

            def shifts(idx, c):
                dve.wait_ge(rstd_ready, idx + 1)
                nc.vector.tensor_tensor(shift[:, c, :], mean[:, c, :], rstd[:, c, :], ALU.mult).then_inc(shift_ready, 1)

            def take(r, c):
                t0 = r % HALVES * HT + c * CH
                dve.wait_ge(chunk_mm, ROUTE_BASE[r] + c + 1)
                nc.vector.tensor_scalar(lg[:, t0:t0 + CH, 0:E], logits_place(r, c)[:, 0:CH * E].rearrange("p (q e) -> p q e", e=E),
                                        LOGIT_CAP, -100.0, ALU.min, ALU.max).then_inc(logits_out, 1)

            def pick(r, c):
                dve.wait_ge(logits_out, r * RC + c + 1)
                t0 = r % HALVES * HT + c * CH
                for t in range(t0, t0 + CH):
                    last = nc.vector.max(top[:, t, 0:2, :].rearrange("p a k -> p (a k)"), lg[:, t, 0:E])
                last.then_inc(top_ready, 1)
                dve.wait_ge(top_ready, r * RC + c + 1)
                me.did(nc.vector.tensor_copy(chosen[:, :, 0, :], top[:, t0:t0 + CH, 0, :]))
                me.wait()
                for q in range(CH):
                    me.did(nc.vector.match_replace(left[:, q, :], chosen[:, q, :, :].rearrange("p a k -> p (a k)"), lg[:, t0 + q, :], NONE))

            def mark(c):
                ts = slice(c * CH, (c + 1) * CH)
                me.wait()
                me.did(nc.vector.tensor_scalar(mask[:, :, ts], left[:, :, 0:E].rearrange("p q e -> p e q"), NONE, None, ALU.is_equal))

            def attend_spread(pair, c):
                dve.wait_ge(combined, pair * HT + (c + 1) * CH)
                spread(ATT_BASE[pair] + c, c % 2, pair * HT + c * CH)

            def slots_of(h, ts):
                for t in range(ts.start, ts.stop):
                    me.did(nc.vector.max(slot[:, t, :], prod[:, :, t]))
                me.wait()
                me.did(nc.vector.tensor_scalar(slot_i[:, ts, :], slot[:, ts, 0:TOP], 1.0, None, ALU.subtract))
                me.did(nc.vector.tensor_scalar(slot_row[:, ts, :], slot[:, ts, 0:TOP], 1.0, float(NG * SG), ALU.subtract, ALU.mult))
                me.wait()
                me.did(nc.vector.tensor_scalar(slot_tile[:, ts, :], slot_i[:, ts, :], P.bit_length() - 1, None,
                                               ALU.arith_shift_right))
                me.wait()
                nc.vector.scalar_tensor_tensor(pos[:, h * HT + ts.start:h * HT + ts.stop, :], slot_tile[:, ts, :],
                                               float(1 - P * NG * SG), slot_row[:, ts, :],
                                               ALU.mult, ALU.add).then_inc(pos_ready, 1)

            def route(r):
                h = r % HALVES
                if r < HALVES:
                    for s in range(RC + 4):
                        if s < RC:
                            dve.wait_ge(x_in[h * RC + s], 16)
                            spread(ROUTE_BASE[r] + s, s % 2, h * HT + s * CH)
                        if 0 <= s - 1 < RC:
                            shifts(ROUTE_BASE[r] + s - 1, (s - 1) % 2)
                        if r == 0 and s == 2:
                            dve.wait_ge(const_ready, 11)
                            nc.vector.memset(lg[:, :, E:E + TOP], NONE)
                            nc.vector.memset(chosen[:, :, :, :], NONE)
                            nc.vector.tensor_copy(iota_k[:, :], iota_ki[:, :])
                            me.did(nc.vector.tensor_copy(iota_j[:, :], iota_ji[:, :]))
                        if s >= 4:
                            take(r, s - 4)
                            pick(r, s - 4)
                            mark(s - 4)
                else:
                    c = RC - 1
                    spread(ROUTE_BASE[r] + c, c % 2, h * HT + c * CH, first=CH - 1)
                    take(r, c - 1)
                    shifts(ROUTE_BASE[r] + c, c % 2)
                    dve.wait_ge(shift_ready, ROUTE_BASE[r] + c + 1)
                    for q in range(CH // 2, CH):
                        last = nc.vector.tensor_scalar(xln[:, h * HT + c * CH + q, :], res[:, h * HT + c * CH + q, :],
                                                       rstd[:, c % 2, q:q + 1], shift[:, c % 2, q:q + 1], ALU.mult, ALU.add)
                    last.then_inc(normed_too, 1)
                    pick(r, c - 1)
                    mark(c - 1)
                    if r == HALVES:
                        combine_next(YR + 2)
                    take(r, c)
                    pick(r, c)
                    mark(c)
                me.wait()
                nc.vector.tensor_tensor_scan(runs[:, :, :].rearrange("p e t -> p (e t)"), restart[:, :, :].rearrange("p e t -> p (e t)"),
                                             mask[:, :, :].rearrange("p e t -> p (e t)"), 0.0,
                                             ALU.mult, ALU.add).then_inc(runs_ready, 1)
                dve.wait_ge(cnt_mm, r + 1)
                me.did(nc.vector.tensor_scalar(cnt_i[:, :], bank67[0:E, 0, 0:1], float(P - 1), None, ALU.add))
                me.wait()
                me.did(nc.vector.tensor_scalar(cnt_s[:, :], cnt_i[:, :], P.bit_length() - 1, None, ALU.arith_shift_right))
                me.wait()
                nc.vector.tensor_copy(tiles_b[:, :], cnt_s[:, :]).then_inc(tiles_ready, 1)
                if r == HALVES:
                    attend_spread(1, 0)
                dve.wait_ge(tiles_ready, r + 1)
                dve.wait_ge(end_mm, r + 1)
                me.did(nc.vector.tensor_copy(end_c[:, :], bank67[0:E, 0, 0:1]))
                me.wait()
                me.did(nc.vector.tensor_tensor(start_c[:, :], end_c[:, :], tiles_b[:, :], ALU.subtract))
                me.did(nc.vector.tensor_scalar(past[:, :], iota_j[:, :], end_c[:, 0:1], None, ALU.is_ge))
                me.wait()
                nc.vector.tensor_scalar(start_d[:, :], ident[0:E, 0:E], start_c[:, 0:1], None, ALU.mult).then_inc(start_ready, 1)
                if r == HALVES:
                    shifts(ATT_BASE[1], 0)
                dve.wait_ge(owner_mm, r + 1)
                nc.vector.tensor_scalar(owner[0:1, h, :], bank67[0:1, 1, 0:NG * SG], float(E - 1), None, ALU.min).then_inc(owner_ready, 1)
                if r == HALVES:
                    attend_spread(1, 1)
                dve.wait_ge(rank_mm, r + 1)
                ranks = bank45[:, :, :].rearrange("p a (e t) -> p (a e) t", t=HT)

                def ranks_of(ts):
                    return nc.vector.scalar_tensor_tensor(prod[:, :, ts], ranks[:, :, ts], 1.0, mask[:, :, ts], ALU.add, ALU.mult)

                me.did(ranks_of(slice(0, CH)))
                if r == HALVES:
                    shifts(ATT_BASE[1] + 1, 1)
                ranks_of(slice(CH, HT)).then_inc(ranks_out, 1)
                if r != HALVES:
                    me.wait()
                    slots_of(h, slice(0, CH))
                    dve.wait_ge(ranks_out, r + 1)
                    slots_of(h, slice(CH, HT))

            def gates(r):
                h = r % HALVES
                for t in range(HT):
                    me.did(nc.vector.max_index(topi[:, t, :], top[:, h * HT + t, 0:2, :].rearrange("p a k -> p (a k)"),
                                               lg[:, h * HT + t, 0:E]))
                me.wait()
                dve.wait_ge(gate_exp, r + 1)
                me.did(nc.vector.tensor_scalar(gk[:, :, :], ge[:, h * HT:(h + 1) * HT, :], 1.0, 2.0, ALU.add, ALU.mult))
                full = [P, HT, TOP, TOP]
                me.did(nc.vector.tensor_tensor(above[:, :, :, :], topi[:, :, 0:TOP].unsqueeze(2).to_broadcast(full),
                                               topi[:, :, 0:TOP].unsqueeze(3).to_broadcast(full), ALU.is_gt))
                me.wait()
                me.did(nc.vector.reciprocal(gk[:, :, :], gk[:, :, :]))
                me.did(nc.vector.tensor_reduce(rank[:, :, :], above[:, :, :, :], AX.X, ALU.add))
                me.wait()
                me.did(nc.vector.tensor_tensor(placed[:, :, :, :], rank[:, :, :].unsqueeze(2).to_broadcast(full),
                                               iota_k[:, :].unsqueeze(1).unsqueeze(3).to_broadcast(full), ALU.is_equal))
                me.wait()
                me.did(nc.vector.tensor_tensor(gsel[:, :, :, :], placed[:, :, :, :], gk[:, :, :].unsqueeze(2).to_broadcast(full),
                                               ALU.mult))
                me.wait()
                nc.vector.tensor_reduce(gate[:, h * HT:(h + 1) * HT, :], gsel[:, :, :, :], AX.X, ALU.add).then_inc(gates_ready, 1)
                dve.wait_ge(gates_ready, r + 1)

            def combine(m, tile, s, ring=None):
                if isinstance(m, int):
                    dve.wait_ge(gathered[s], 16 * TOP * (m // 2 + 1))
                    rows = yg[:, m % YR, :, :]
                else:
                    dve.wait_ge(gathered[s], m * (16 * TOP // 2) + (2 - s) * (16 * TOP // 2))
                    rows = yg[:, bass.ds(ring, 1), :, :].rearrange("p o k d -> p (o k) d")
                for k in range(TOP):
                    ins = nc.vector.scalar_tensor_tensor(
                        tile_of(res, tile), rows[:, k, :], gate[:, bass.ds(tile, 1), k:k + 1].rearrange("p o d -> p (o d)"),
                        tile_of(res, tile), ALU.mult, ALU.add)
                    if k < TOP - 1:
                        me.did(ins)
                        me.wait()
                    else:
                        ins.then_inc(combined, 1)

            def combine_two(m):
                for u in (m, m + 1):
                    dve.wait_ge(gathered[u % 2], 16 * TOP * (u // 2 + 1))
                start = me.count
                for k in range(TOP):
                    for u in (m, m + 1):
                        if k:
                            dve.wait_ge(dve_self, start + 2 * k - 1 + u - m)
                        ins = nc.vector.scalar_tensor_tensor(res[:, u, :], yg[:, u % YR, k, :], gate[:, u, k:k + 1],
                                                             res[:, u, :], ALU.mult, ALU.add)
                        if k < TOP - 1:
                            me.did(ins)
                        else:
                            ins.then_inc(combined, 1)

            owner_regs = [[dve.alloc_register(f"dve_owner{r}_{q}") for q in range(2 * SG)] for r in range(ROUTES)]

            def experts(r, begin=True, rest=True):
                h = r % HALVES
                regs = owner_regs[r]
                dve.wait_ge(owner_ready, r + 1)
                if r == 0:
                    dve.wait_ge(keys_loaded, 16)

                def stage(n, s, g):
                    if s % 2 == 0:
                        dve.load(regs, owner[0:1, h, bass.ds(g * SG, 2 * SG)])
                    if not isinstance(n, int) or n >= UN:
                        dve.wait_ge(h_mm, n - (UN - 1))
                    for q in range(SG):
                        e = dve.snap(regs[s % 2 * SG + q], min_val=0, max_val=E - 1)
                        last = nc.vector.tensor_copy(wk[:, s, q, :], keys_sb[:, bass.ds(e, 1), :].rearrange("p o d -> p (o d)"))
                    last.then_inc(keys_staged, 1)

                def step(g, n, u):
                    if g is None or g + 2 < NG:
                        stage(n + 2, (u + 2) % UN, n - r * NG + 2)
                    if h == 1 and u % 2 == 1 and (g is None or g >= 0):
                        tile_after(g, n, u)

                def tile_after(g, n, u):
                    if g is None:
                        t = loop_turn[0] * (UN // 2) + (u // 2 - LAG)
                        combine(t + (r - 1) * HT, t, (u // 2 - LAG) % 2, t % YR)
                    elif g // 2 >= LAG:
                        t = g // 2 - LAG
                        combine((r - 1) * HT + t, t, t % 2)

                if begin:
                    step(-2, r * NG - 2, -2)
                    step(-1, r * NG - 1, -1)
                if not rest:
                    return
                loop_turn = [None]
                first_turn = 1 if r == 0 or h == 1 else 0
                for g in range(first_turn * UN):
                    step(g, r * NG + g, g)
                turns = NG // UN - 1 - first_turn
                per_turn = (UN // 2) * (TOP - 1) if h == 1 else 0
                n_before = me.count
                with dve.Fori(first_turn, first_turn + turns) as i:
                    loop_turn[0] = i
                    me.loop_part = i * per_turn - first_turn * per_turn if per_turn else None
                    for u in range(UN):
                        step(None, i * UN + (r * NG + u), u)
                me.loop_part = None
                assert me.count - n_before == per_turn
                me.count += per_turn * (turns - 1)
                for g in range(NG - UN, NG):
                    step(g, r * NG + g, g)
                    if r == 1 and g == NG - 2:
                        attend_spread(0, 0)

            def attend(pair, between):
                place_v = (bank23[:, 1, :], bank67[:, 0, :])

                def values_out(c):
                    n = 2 * BC * pair + c
                    dve.wait_ge(chunk_mm, ATT_BASE[pair] + c + 1)
                    nc.vector.tensor_tensor(V[:, c // BC, (c % BC) * CH:(c % BC + 1) * CH, :],
                                            place_v[c % 2].rearrange("p (q d) -> p q d", d=D),
                                            bv_r[:, :].unsqueeze(1).to_broadcast([P, CH, D]), ALU.add).then_inc(v_ready, 1)

                if pair == 0:
                    for c in range(2 * BC + 1):
                        if c == 2 * BC - 1:
                            for t in range(HT - LAG, HT, 2):
                                combine_two(t)
                        if 0 < c < 2 * BC:
                            attend_spread(pair, c)
                        if c > 0:
                            shifts(ATT_BASE[pair] + c - 1, (c - 1) % 2)
                    values_out(0)
                    values_out(1)
                    between(-2)
                    values_out(2)
                    values_out(3)
                    between(-1)
                else:
                    combine_next(3 * CH)
                    attend_spread(pair, 2)
                    slots_of(0, slice(0, CH))
                    combine_next(3 * CH + 2)
                    shifts(ATT_BASE[pair] + 2, 0)
                    values_out(0)
                    combine_next(4 * CH)
                    attend_spread(pair, 3)
                    shifts(ATT_BASE[pair] + 3, 1)
                    dve.wait_ge(ranks_out, HALVES + pair)
                    slots_of(0, slice(CH, HT))
                    for c in range(1, 2 * BC):
                        values_out(c)

                def largest(j):
                    dve.wait_ge(s_mm, pair * 2 * BT + j + 1)
                    src = (bank45, bank67)[j % 2][:, :, :].rearrange("p a n -> p (a n)")
                    nc.vector.tensor_reduce(nmax[:, j % 2, :], src[:, 0:(j % BT + 1) * P], AX.X, ALU.max,
                                            negate=True).then_inc(max_ready, 1)

                r = HALVES + pair

                def alongside(j):
                    def spread_chunk(c):
                        dve.wait_ge(z_added, (pair * RC + c + 1) * CH)
                        spread(ROUTE_BASE[r] + c, c % 2, pair * HT + c * CH)

                    if j == BT - 4:
                        spread_chunk(0)
                    elif j == BT - 3:
                        shifts(ROUTE_BASE[r], 0)
                    elif j == BT - 1:
                        spread_chunk(1)
                    elif j == BT:
                        shifts(ROUTE_BASE[r] + 1, 1)
                    elif j == BT + 1:
                        take(r, 0)
                    elif j == BT + 2:
                        take(r, 1)
                        pick(r, 0)
                        mark(0)
                    elif j == BT + 3:
                        spread_chunk(2)
                    elif j == BT + 4:
                        shifts(ROUTE_BASE[r] + 2, 0)
                    elif j == BT + 5:
                        pick(r, 1)
                        mark(1)
                    elif j == 2 * BT - 2:
                        dve.wait_ge(z_added, (pair + 1) * HT - 1)
                        spread_rows((RC - 1) % 2, (pair + 1) * HT - CH, range(CH - 1))

                largest(0)
                largest(1)
                for j in range(2 * BT):
                    z = pair * 2 * BT + j
                    if j + 2 < 2 * BT:
                        largest(j + 2)
                    if j < 2:
                        dve.wait_ge(exp_ready, z + 1)
                    me.did(nc.vector.reciprocal(rinv[:, j % 2, :], rowsum[:, j % 4, :]))
                    me.wait()
                    dve.wait_ge(z_mm, z + 1)
                    nc.vector.scalar_tensor_tensor(res[:, z, :], bank23[:, j % 2, 0:D], rinv[:, j % 2, :], res[:, z, :],
                                                   ALU.mult, ALU.add).then_inc(z_added, 1)
                    between(j)
                    alongside(j)
                dve.wait_ge(z_added, 2 * BT * (pair + 1))

            done = [0]

            def combine_next(upto_n):
                while done[0] + 2 <= min(upto_n, HT):
                    combine_two(HT + done[0])
                    done[0] += 2

            route(0)
            gates(0)
            route(1)
            gates(1)
            experts(0)
            experts(1)
            attend(0, lambda j: combine_next(min(4 + j // 3 * 2, YR)))
            route(2)
            attend(1, lambda j: experts(2, rest=False) if j == 2 * BT - 3 else None)
            route(3)
            experts(2, begin=False)
            gates(2)
            experts(3)
            gates(3)
            for t in range(HT - LAG, HT):
                combine(2 * HT + t, t, t % 2)
            for t in range(HT):
                combine(3 * HT + t, HT + t, t % 2)


_INS = ['L0_attn_x', 'L0_attn_Wq', 'L0_attn_bq', 'L0_attn_Wk', 'L0_attn_bk', 'L0_attn_Wv', 'L0_attn_bv',
        'L0_ffn_expert_sel', 'L0_ffn_keys', 'L0_ffn_values']


def kernel(**inputs):
    import numpy as _np
    import concourse.bacc as _bacc
    from concourse import mybir as _mybir
    from concourse.bass_utils import run_bass_kernel_spmd as _run

    nc = _bacc.Bacc("TRN2", target_bir_lowering=False, num_devices=1)
    arrays, args = {}, []
    for name in _INS:
        a = _np.ascontiguousarray(inputs[name])
        arrays[f"in_{name}_dram"] = a
        args.append(nc.dram_tensor(f"in_{name}_dram", a.shape, _mybir.dt.from_np(a.dtype), kind="ExternalInput").ap())
    shape = inputs['L0_attn_x'].shape
    out = nc.dram_tensor("out_0_dram", shape, _mybir.dt.float32, kind="ExternalOutput").ap()
    moe_attention_macaron_kernel(nc, *args, out)
    r = _run(nc, [arrays], core_ids=[0])
    return r.results[0]["out_0_dram"]
```
